# Optimizing a Trainium2 kernel written in Bass

```python
import numpy as np
import jax
import jax.numpy as jnp

def _softmax(x, axis=-1):
    return jax.nn.softmax(x, axis=axis)

def _gelu(x):
    return jax.nn.gelu(x, approximate=True)

def _silu(x):
    return jax.nn.silu(x)

def _sigmoid(x):
    return jax.nn.sigmoid(x)

def _layernorm(x, axis=-1, eps=1e-05):
    m = jnp.mean(x, axis=axis, keepdims=True)
    v = jnp.var(x, axis=axis, keepdims=True)
    return (x - m) / jnp.sqrt(v + eps)

def _scatter_add(tgt, idx, src, axis=0):
    return tgt.at[idx].add(src)

def _segment_sum(src, seg, n):
    return jax.ops.segment_sum(src, seg, n)
kernel_name = 'mk_perceiver_d1_seqx_r4_ab7ae9'

def setup_inputs(seed: int=0):
    np.random.seed(seed)
    _w = jnp.asarray

    def _rec_inputs():
        import jax
        import jax.numpy as jnp
        _rk = jax.random.key(seed)
        x = -0.0003929 + 0.9999 * jax.random.normal(jax.random.fold_in(_rk, 1), (1, 128, 256), jnp.float32)
        _lenS = 128 - jax.random.randint(jax.random.fold_in(_rk, 7), (1,), 0, max(1, 128 // 4) + 1, jnp.int32)
        _lenS2 = 12544 - jax.random.randint(jax.random.fold_in(_rk, 8), (1,), 0, max(1, 12544 // 4) + 1, jnp.int32)
        _ctx_1024P = jax.random.normal(jax.random.fold_in(_rk, 11), (1, 16, 256), jnp.float32)
        _ctx_1024c = jax.random.dirichlet(jax.random.fold_in(_rk, 511), 0.3 * jnp.ones((16,), jnp.float32), (1, 12544))
        _ctx_1024t = jnp.einsum('bsk,bkd->bsd', _ctx_1024c, _ctx_1024P)
        _ctx_1024t = _ctx_1024t * jax.lax.rsqrt(jnp.mean(jnp.square(_ctx_1024t)) + 1e-12) * 0.953939
        ctx_1024 = 2.81802e-05 + 1.00001 * (_ctx_1024t + 0.3 * jax.random.normal(jax.random.fold_in(_rk, 611), (1, 12544, 256), jnp.float32))
        return (x, ctx_1024)
    x, ctx_1024 = _rec_inputs()

    def _L0_xattn_setup():
        import jax, jax.numpy as jnp
        import numpy as np
        key = jax.random.key(seed)
        k1, k2, k3, k4 = jax.random.split(key, 4)
        B, L1, L2, D = (32, 128, 128, 256)
        ix = jax.random.normal(k1, (B, L1, D), dtype=jnp.float32)
        iother = jax.random.normal(k2, (B, L2, D), dtype=jnp.float32)
        scale = 1.0 / np.sqrt(D)
        W = jax.random.uniform(k3, (D, D), dtype=jnp.float32, minval=-scale, maxval=scale)
        b = jax.random.uniform(k4, (D,), dtype=jnp.float32, minval=-scale, maxval=scale)
        return {'ix': ix, 'iother': iother, 'W': W, 'b': b}
    _L0_xattn_all = _L0_xattn_setup()
    _L0_xattn_in = {k: v for k, v in _L0_xattn_all.items() if k in ('W', 'b')}
    del _L0_xattn_all

    def _L0_attn_setup():
        import jax, jax.numpy as jnp
        import numpy as np
        D_MODEL = 256
        MAX_LEN = 512
        ORDER = 2
        BATCH = 4
        SEQ = 512
        key = jax.random.key(seed)
        k1, k2, k3, k4 = jax.random.split(key, 4)
        x = jax.random.normal(k1, (BATCH, SEQ, D_MODEL), dtype=jnp.float32)
        proj_w = jax.random.normal(k2, (D_MODEL, D_MODEL * (ORDER + 1)), dtype=jnp.float32) * D_MODEL ** (-0.5)
        proj_b = jax.random.normal(k3, (D_MODEL * (ORDER + 1),), dtype=jnp.float32) * 0.02
        filter_time = jax.random.normal(k4, (ORDER, 1, MAX_LEN, D_MODEL), dtype=jnp.float32) / MAX_LEN ** 0.5
        return {'x': x, 'proj_w': proj_w, 'proj_b': proj_b, 'filter_time': filter_time}
    _L0_attn_all = _L0_attn_setup()
    _L0_attn_in = {k: v for k, v in _L0_attn_all.items() if k in ('proj_w', 'proj_b', 'filter_time')}
    del _L0_attn_all

    def _L0_ffn_setup():
        import jax, jax.numpy as jnp
        import numpy as np
        B, N, D = (4, 1024, 256)
        E, S, F = (16, 64, 512)
        DO = 256
        EPS = 1e-05

        def _layernorm(x, g, b):
            mu = jnp.mean(x, axis=-1, keepdims=True)
            var = jnp.mean(jnp.square(x - mu), axis=-1, keepdims=True)
            return (x - mu) * jax.lax.rsqrt(var + EPS) * g + b
        key = jax.random.key(seed)
        ks = jax.random.split(key, 8)
        d = {'x': jax.random.normal(ks[0], (B, N, D), dtype=jnp.float32), 'norm_g': jnp.ones((D,), jnp.float32), 'norm_b': jnp.zeros((D,), jnp.float32), 'slot_g': jnp.ones((D,), jnp.float32), 'slot_b': jnp.zeros((D,), jnp.float32), 'scale': jnp.ones((1,), jnp.float32), 'slot_embeds': jax.random.normal(ks[1], (E, S, D), jnp.float32) / np.sqrt(D), 'Wg': jax.random.normal(ks[2], (E, D, F), jnp.float32) * np.sqrt(2.0 / (D + F)), 'bg': jnp.zeros((E, F), jnp.float32), 'Wu': jax.random.normal(ks[3], (E, D, F), jnp.float32) * np.sqrt(2.0 / (D + F)), 'bu': jnp.zeros((E, F), jnp.float32), 'Wd': jax.random.normal(ks[4], (E, F, DO), jnp.float32) * np.sqrt(2.0 / (F + DO)), 'bd': jnp.zeros((E, DO), jnp.float32)}
        return d
    _L0_ffn_all = _L0_ffn_setup()
    _L0_ffn_in = {k: v for k, v in _L0_ffn_all.items() if k in ('norm_g', 'norm_b', 'slot_g', 'slot_b', 'scale', 'slot_embeds', 'Wg', 'bg', 'Wu', 'bu', 'Wd', 'bd')}
    del _L0_ffn_all
    return {'x': x, 'ctx_1024': ctx_1024, 'L0_xattn_W': _L0_xattn_in['W'], 'L0_xattn_b': _L0_xattn_in['b'], 'L0_attn_proj_w': _L0_attn_in['proj_w'], 'L0_attn_proj_b': _L0_attn_in['proj_b'], 'L0_attn_filter_time': _L0_attn_in['filter_time'], 'L0_ffn_norm_g': _L0_ffn_in['norm_g'], 'L0_ffn_norm_b': _L0_ffn_in['norm_b'], 'L0_ffn_slot_g': _L0_ffn_in['slot_g'], 'L0_ffn_slot_b': _L0_ffn_in['slot_b'], 'L0_ffn_scale': _L0_ffn_in['scale'], 'L0_ffn_slot_embeds': _L0_ffn_in['slot_embeds'], 'L0_ffn_Wg': _L0_ffn_in['Wg'], 'L0_ffn_bg': _L0_ffn_in['bg'], 'L0_ffn_Wu': _L0_ffn_in['Wu'], 'L0_ffn_bu': _L0_ffn_in['bu'], 'L0_ffn_Wd': _L0_ffn_in['Wd'], 'L0_ffn_bd': _L0_ffn_in['bd']}

def reference(x, ctx_1024, L0_xattn_W, L0_xattn_b, L0_attn_proj_w, L0_attn_proj_b, L0_attn_filter_time, L0_ffn_norm_g, L0_ffn_norm_b, L0_ffn_slot_g, L0_ffn_slot_b, L0_ffn_scale, L0_ffn_slot_embeds, L0_ffn_Wg, L0_ffn_bg, L0_ffn_Wu, L0_ffn_bu, L0_ffn_Wd, L0_ffn_bd):
    import jax
    import jax.numpy as jnp

    def _L0_xattn_ref(ix, iother, W, b):
        import jax, jax.numpy as jnp
        import numpy as np
        ex = jnp.einsum('bld,ed->ble', ix, W) + b
        eother = jnp.einsum('bld,ed->ble', iother, W) + b
        scores = jnp.einsum('bld,bmd->blm', ex, eother)
        attn = jax.nn.softmax(scores, axis=-1)
        aligned = jnp.einsum('blm,bmd->bld', attn, iother)
        return aligned

    def _L0_attn_ref(x, proj_w, proj_b, filter_time):
        import jax, jax.numpy as jnp
        import numpy as np
        D_MODEL = 256
        MAX_LEN = 512
        ORDER = 2
        BATCH = 4
        SEQ = 512
        B, L, D = x.shape
        order, _, max_length, _ = filter_time.shape
        fft_size = 2 * max_length
        p = (jnp.einsum('bld,de->ble', x, proj_w) + proj_b).reshape(B, L, order + 1, D)
        v = p[:, :, 0, :]
        for stage in range(order):
            vf = jnp.fft.rfft(v, n=fft_size, axis=1)
            ff = jnp.fft.rfft(filter_time[stage], n=fft_size, axis=1)
            conv = jnp.fft.irfft(vf * ff, n=fft_size, axis=1)[:, :L, :]
            v = conv * p[:, :, stage + 1, :]
        return v

    def _L0_ffn_ref(x, norm_g, norm_b, slot_g, slot_b, scale, slot_embeds, Wg, bg, Wu, bu, Wd, bd):
        import jax, jax.numpy as jnp
        import numpy as np
        B, N, D = (4, 1024, 256)
        E, S, F = (16, 64, 512)
        DO = 256
        EPS = 1e-05

        def _layernorm(x, g, b):
            mu = jnp.mean(x, axis=-1, keepdims=True)
            var = jnp.mean(jnp.square(x - mu), axis=-1, keepdims=True)
            return (x - mu) * jax.lax.rsqrt(var + EPS) * g + b
        x = _layernorm(x, norm_g, norm_b)
        se = _layernorm(slot_embeds, slot_g, slot_b) * scale
        logits = jnp.einsum('bnd,esd->bnes', x, se)
        dispatch = jax.nn.softmax(logits, axis=1)
        combine = jax.nn.softmax(logits.reshape(x.shape[0], x.shape[1], -1), axis=-1)
        slots = jnp.einsum('bnd,bnes->besd', x, dispatch)
        gate = jax.nn.gelu(jnp.einsum('besd,edf->besf', slots, Wg) + bg[None, :, None, :], approximate=False)
        up = jnp.einsum('besd,edf->besf', slots, Wu) + bu[None, :, None, :]
        eout = jnp.einsum('besf,efo->beso', gate * up, Wd) + bd[None, :, None, :]
        eout = eout.reshape(eout.shape[0], -1, eout.shape[-1])
        return jnp.einsum('bns,bso->bno', combine, eout)
    x = x + _L0_xattn_ref(_layernorm(x, axis=-1), ctx_1024, L0_xattn_W, L0_xattn_b)
    x = x + _L0_attn_ref(_layernorm(x, axis=-1), L0_attn_proj_w, L0_attn_proj_b, L0_attn_filter_time)
    x = x + _L0_ffn_ref(_layernorm(x, axis=-1), L0_ffn_norm_g, L0_ffn_norm_b, L0_ffn_slot_g, L0_ffn_slot_b, L0_ffn_scale, L0_ffn_slot_embeds, L0_ffn_Wg, L0_ffn_bg, L0_ffn_Wu, L0_ffn_bu, L0_ffn_Wd, L0_ffn_bd)
    return x

_drawn_inputs = setup_inputs


def setup_inputs(seed=0):
    import zlib

    import numpy as np

    out = dict(_drawn_inputs(seed))
    spreads = {'L0_ffn_norm_g': (1.0, 0.2),
     'L0_ffn_norm_b': (0.0, 0.1),
     'L0_ffn_slot_g': (1.0, 0.2),
     'L0_ffn_slot_b': (0.0, 0.1),
     'L0_ffn_bg': (0.0, 0.1),
     'L0_ffn_bu': (0.0, 0.1),
     'L0_ffn_bd': (0.0, 0.1)}
    factors = {'L0_attn_proj_b': 24.55}
    for name, (base, spread) in spreads.items():
        noise = np.random.default_rng([zlib.crc32(name.encode()), seed]).standard_normal(out[name].shape)
        drawn = base * np.exp(spread * noise) if base else spread * noise
        out[name] = jnp.asarray(drawn.astype(out[name].dtype))
    for name, factor in factors.items():
        out[name] = (out[name] * factor).astype(out[name].dtype)
    return out
```

```python
import concourse.bass as bass
from concourse import mybir
from contextlib import ExitStack


def perceiver_kernel(nc, x, ctx_in, xattn_W, xattn_b, proj_w, proj_b, filter_time, norm_g, norm_b,
                     slot_g, slot_b, scale, slot_embeds, Wg, bg, Wu, bu, Wd, bd, columns, tables, out):
    fp32 = mybir.dt.float32
    fp32r = mybir.dt.float32r
    ALU = mybir.AluOpType
    ACT = mybir.ActivationFunctionType
    AX = mybir.AxisListType

    P = 128
    D = x.shape[2]
    DK = D // P
    KEYS = ctx_in.shape[1]
    TILES = KEYS // P
    GT = 4
    GROUPS = -(-TILES // GT)
    LAST = GROUPS - 1
    LAST_T = TILES - LAST * GT
    RING = 4
    LOOPS = (GROUPS - 5) // RING
    FIRST = 3
    ORDER = filter_time.shape[0]
    E, SL = slot_embeds.shape[0], slot_embeds.shape[1]
    F = Wg.shape[2]
    FC = F // P
    PAIRS = E * SL // P
    SLOTS = E * SL
    WSLOTS = 3
    EPS = 1e-5
    BIG = 3.0e38

    def tiles_of(g):
        return LAST_T if g == LAST else GT

    st = ExitStack()
    with st:
        def sem(name):
            return st.enter_context(nc.semaphore(name))

        def sb(name, shape, dt=fp32, where=st):
            return where.enter_context(nc.sbuf_tensor(name, shape, dt))

        bank = [st.enter_context(nc.psum_tensor(f"bank{i}", [P, 512], fp32)) for i in range(8)]

        tab = sb("tab", [P, 5, P])
        ident, dft_c, dft_s, inv_c, inv_s = (tab[:, i, :] for i in range(5))
        x_sb = sb("x_sb", [P, D])
        x1 = sb("x1", [P, D])
        x2 = sb("x2", [P, D])
        xh = sb("xh", [P, D])
        xhT = sb("xhT", [P, DK, P])
        xn = sb("xn", [P, D])
        xnT = sb("xnT", [P, DK, P])
        stat6 = sb("stat6", [P, 6])
        mv = sb("mv", [P, 2])
        rstd = sb("rstd", [P, 1])
        neg_half = sb("neg_half", [P, PAIRS])
        zero = sb("zero", [P, 1])
        col = sb("col", [P, 5, DK])
        scale_b = sb("scale_b", [P, 1])
        g_row = sb("g_row", [P, 2, D])
        pw = sb("pw", [P, DK, 3 * D])
        pb = sb("pb", [P, 3 * D])
        filt = sb("filt", [P, ORDER, D])
        spec = sb("spec", [P, ORDER, 3, D])
        seT = sb("seT", [P, DK, SLOTS])
        negm = sb("negm", [P, RING])
        ebias = sb("ebias", [P, RING])
        gmax = sb("gmax", [P, 1])
        rsum = sb("rsum", [P, RING])
        alpha = sb("alpha", [P, RING])
        s0 = sb("s0", [P, 1])
        lsum = sb("lsum", [P, 1])
        linv = sb("linv", [P, 1])
        O = sb("O", [P, D])
        w_gu = [sb(f"w_gu{i}", [P, 2, 2, DK, F]) for i in range(2)]
        w_d = [sb(f"w_d{i}", [P, 2, FC, D]) for i in range(2)]
        bias_gu = sb("bias_gu", [P, 2, 2, F])
        bias_d = sb("bias_d", [P, 2, D])

        att = ExitStack()
        raw = sb("raw", [P, RING, GT, D], fp32, att)
        c_hi = sb("c_hi", [P, RING, GT, D], fp32r, att)
        c_lo = sb("c_lo", [P, RING, GT, D], fp32r, att)
        cT_hi = sb("cT_hi", [P, 2, DK, GT * P], fp32r, att)
        cT_lo = sb("cT_lo", [P, 2, DK, GT * P], fp32r, att)
        prob = sb("prob", [P, 2, GT * P], fp32, att)
        pT_hi = sb("pT_hi", [P, 2, GT * P], fp32r, att)
        pT_lo = sb("pT_lo", [P, 2, GT * P], fp32r, att)
        q_hi = sb("q_hi", [P, DK, P], fp32r, att)
        q_lo = sb("q_lo", [P, DK, P], fp32r, att)
        att.close()
        pre = ExitStack()
        sb("under_raw", [P, RING, GT, D], fp32, pre)
        se = sb("se", [P, PAIRS, D], fp32, pre)
        W_sb = sb("W_sb", [P, DK, D], fp32, pre)
        WT = sb("WT", [P, DK, D], fp32, pre)
        exT = sb("exT", [P, DK, P], fp32, pre)
        se_stat = sb("se_stat", [P, PAIRS, 6], fp32, pre)
        se_mv = sb("se_mv", [P, PAIRS, 2], fp32, pre)
        se_rstd = sb("se_rstd", [P, PAIRS], fp32, pre)
        pre.close()
        ffn = ExitStack()
        w_gu.append(sb("w_gu2", [P, 2, 2, DK, F], fp32, ffn))
        w_d.append(sb("w_d2", [P, 2, FC, D], fp32, ffn))
        p_sb = sb("p_sb", [P, 3 * D], fp32, ffn)
        vbuf = sb("vbuf", [P, 2, D], fp32, ffn)
        prod = sb("prod", [P, 2, 2 * D], fp32, ffn)
        dT = sb("dT", [P, PAIRS, P], fp32, ffn)
        disp = sb("disp", [P, SLOTS], fp32, ffn)
        comb = sb("comb", [P, SLOTS], fp32, ffn)
        combT = sb("combT", [P, PAIRS, P], fp32, ffn)
        slotsT = sb("slotsT", [P, DK, SLOTS], fp32, ffn)
        gate = sb("gate", [P, 2, F], fp32, ffn)
        up = sb("up", [P, F], fp32, ffn)
        hid = sb("hid", [P, F], fp32, ffn)
        hidT = sb("hidT", [P, FC, P], fp32, ffn)
        eout = sb("eout", [P, D], fp32, ffn)
        cmax = sb("cmax", [P, PAIRS], fp32, ffn)
        csum = sb("csum", [P, PAIRS], fp32, ffn)
        cinv = sb("cinv", [P, PAIRS], fp32, ffn)
        rmax = sb("rmax", [P, 3], fp32, ffn)
        rs = sb("rs", [P, 4], fp32, ffn)
        ffn.close()

        ld_x, ld_W, ld_tab, ld_scale = sem("ld_x"), sem("ld_W"), sem("ld_tab"), sem("ld_scale")
        ld_se, ld_col, ld_row, ld_filt = sem("ld_se"), sem("ld_col"), sem("ld_row"), sem("ld_filt")
        ld_pw = sem("ld_pw")
        ld_raw = [sem(f"ld_raw{i}") for i in range(RING)]
        ld_wgu = [sem(f"ld_wgu{i}") for i in range(WSLOTS)]
        ld_wd = [sem(f"ld_wd{i}") for i in range(WSLOTS)]
        ld_bias = [sem(f"ld_bias{i}") for i in range(2)]
        st_out = sem("st_out")
        dve_n = sem("dve_n")
        half_set = sem("half_set")
        var_rdy, rstd_rdy = sem("var_rdy"), sem("rstd_rdy")
        xh_rdy, xhT_ps, xhT_rdy = sem("xh_rdy"), sem("xhT_ps"), sem("xhT_rdy")
        WT_ps, WT_rdy = sem("WT_ps"), sem("WT_rdy")
        exT_ps, exT_rdy = sem("exT_ps"), sem("exT_rdy")
        q_ps, qhi_rdy, q_rdy, s0_rdy = sem("q_ps"), sem("qhi_rdy"), sem("q_rdy"), sem("s0_rdy")
        se_rdy, seT_ps, seT_rdy = sem("se_rdy"), sem("seT_ps"), sem("seT_rdy")
        gs_rdy = sem("gs_rdy")
        spec_ps, spec_rdy = sem("spec_ps"), sem("spec_rdy")
        cT_ps, cThi_rdy, cTlo_rdy = sem("cT_ps"), sem("cThi_rdy"), sem("cTlo_rdy")
        score_ps, gmax_rdy, negm_rdy, ebias_rdy = (sem("score_ps"), sem("gmax_rdy"), sem("negm_rdy"),
                                                   sem("ebias_rdy"))
        prob_rdy, alpha_rdy = sem("prob_rdy"), sem("alpha_rdy")
        pT_ps, pThi_rdy, pTlo_rdy = sem("pT_ps"), sem("pThi_rdy"), sem("pTlo_rdy")
        chi_rdy, clo_rdy = sem("chi_rdy"), sem("clo_rdy")
        pv_ps, O_upd, l_upd = sem("pv_ps"), sem("O_upd"), sem("l_upd")
        proj_ps, v_rdy, freq_ps = sem("proj_ps"), sem("v_rdy"), sem("freq_ps")
        prod_rdy, conv_ps = sem("prod_rdy"), sem("conv_ps")
        x2_rdy, z_rdy, zT_ps, xn_rdy, xnT_rdy = (sem("x2_rdy"), sem("z_rdy"), sem("zT_ps"),
                                                 sem("xn_rdy"), sem("xnT_rdy"))
        LT_ps, L_ps = sem("LT_ps"), sem("L_ps")
        cmax_rdy, dexp_rdy, dT_rdy = sem("cmax_rdy"), sem("dexp_rdy"), sem("dT_rdy")
        disp_ps, disp_rdy = sem("disp_ps"), sem("disp_rdy")
        slots_ps, slots_rdy = sem("slots_ps"), [sem(f"slots_rdy{k}") for k in range(DK)]
        rmax_rdy, cexp_rdy = sem("rmax_rdy"), sem("cexp_rdy")
        combT_ps, combT_rdy = sem("combT_ps"), sem("combT_rdy")
        gate_ps, up_ps, gate_rdy, up_rdy = sem("gate_ps"), sem("up_ps"), sem("gate_rdy"), sem("up_rdy")
        gelu_rdy, hid_rdy, hidT_ps, hidT_rdy = (sem("gelu_rdy"), sem("hid_rdy"), sem("hidT_ps"),
                                                sem("hidT_rdy"))
        down_ps, eout_rdy, mix_ps, res_rdy = sem("down_ps"), sem("eout_rdy"), sem("mix_ps"), sem("res_rdy")

        ctx_v = ctx_in[0, :, :].rearrange("(p j) d -> p j d", p=P)

        def times(loop, static):
            return static if loop is None else loop * RING + static

        def twice(loop, static):
            return static if loop is None else loop * (2 * RING) + static

        def raw_count(loop, g):
            n = 16 * (g // RING + 1)
            return n if loop is None else loop * 16 + n

        def load_bias(eng, p):
            s = p % 2
            for a in range(2):
                for i, b in enumerate((bg, bu)):
                    eng.dma_start(bias_gu[a * SL:(a + 1) * SL, s, i, :],
                                  b[2 * p + a:2 * p + a + 1, :].broadcast_to([SL, F])).then_inc(ld_bias[s], 16)
                eng.dma_start(bias_d[a * SL:(a + 1) * SL, s, :],
                              bd[2 * p + a:2 * p + a + 1, :].broadcast_to([SL, D])).then_inc(ld_bias[s], 16)
        BIAS_LOADS = 6 * 16

        def transpose_xh(pe, n):
            pe.wait_ge(xh_rdy, n + 1)
            for k in range(DK):
                last = nc.tensor.transpose(bank[1][:, k * P:(k + 1) * P], xh[:, k * P:(k + 1) * P], ident)
            last.then_inc(xhT_ps, 1)

        block = st.enter_context(nc.Block())

        @block.sync
        def _(sp):
            sp.dma_start(x_sb[:, :], x[0, :, :]).then_inc(ld_x, 16)
            sp.dma_start(W_sb[:, :, :], xattn_W.rearrange("(k p) d -> p k d", p=P)).then_inc(ld_W, 16)
            sp.dma_start(tab[:, :, :], tables).then_inc(ld_tab, 16)
            sp.dma_start(col[:, :, :], columns).then_inc(ld_col, 16)
            for g in range(2):
                sp.dma_start(raw[:, g, :, :], ctx_v[:, g * GT:(g + 1) * GT, :]).then_inc(ld_raw[g], 16)
            sp.dma_start(se[:, :, :], slot_embeds.rearrange("(j a) s d -> (a s) j d", a=2)).then_inc(ld_se, 16)
            for g in range(2, RING):
                sp.dma_start(raw[:, g, :, :], ctx_v[:, g * GT:(g + 1) * GT, :]).then_inc(ld_raw[g], 16)
            with sp.Fori(0, LOOPS) as n:
                for u in range(RING):
                    sp.wait_ge(score_ps, n * RING + (u + 1))
                    sp.wait_ge(clo_rdy, n * RING + (u + 1))
                    sp.dma_start(raw[:, u, :, :], ctx_v[:, bass.ds(n * (RING * GT) + (RING + u) * GT, GT), :]
                                 ).then_inc(ld_raw[u], 16)
            u = LAST % RING
            sp.wait_ge(score_ps, LAST - RING + 1)
            sp.wait_ge(clo_rdy, LAST - RING + 1)
            sp.dma_start(raw[:, u, 0:LAST_T, :], ctx_v[:, LAST * GT:TILES, :]).then_inc(ld_raw[u], 16)
            for p in range(WSLOTS - 1, PAIRS):
                s = p % WSLOTS
                if p == WSLOTS - 1:
                    sp.wait_ge(pv_ps, GROUPS)
                else:
                    sp.wait_ge(up_ps, p - WSLOTS + 1)
                for i, w in enumerate((Wg, Wu)):
                    sp.dma_start(w_gu[s][:, i, :, :, :].rearrange("p e k f -> p (e k) f"),
                                 w[2 * p:2 * p + 2, :, :].rearrange("e (k p) f -> p (e k) f", p=P)
                                 ).then_inc(ld_wgu[s], 16)
                if p >= WSLOTS:
                    sp.wait_ge(down_ps, p - WSLOTS + 1)
                sp.dma_start(w_d[s][:, :, :, :].rearrange("p e c o -> p (e c) o"),
                             Wd[2 * p:2 * p + 2, :, :].rearrange("e (c p) o -> p (e c) o", p=P)
                             ).then_inc(ld_wd[s], 16)
            sp.wait_ge(res_rdy, 1)
            sp.dma_start(out[0, :, :], x1[:, :]).then_inc(st_out, 16)
            sp.wait_ge(st_out, 16)

        @block.tensor
        def _(pe):
            pe.wait_ge(ld_tab, 16)
            pe.wait_ge(ld_W, 16)
            for d in range(DK):
                for e in range(DK):
                    last = nc.tensor.transpose(bank[0][:, (2 * d + e) * P:(2 * d + e + 1) * P],
                                               W_sb[:, e, d * P:(d + 1) * P], ident)
            last.then_inc(WT_ps, 1)
            transpose_xh(pe, 0)
            pe.wait_ge(WT_rdy, 1)
            pe.wait_ge(xhT_rdy, 1)
            for e in range(DK):
                for d in range(DK):
                    last = nc.tensor.matmul(bank[2][:, e * P:(e + 1) * P], WT[:, d, e * P:(e + 1) * P],
                                            xhT[:, d, :], start=(d == 0), stop=(d == DK - 1))
            last.then_inc(exT_ps, 1)
            pe.wait_ge(exT_rdy, 1)
            for d in range(DK):
                for e in range(DK):
                    nc.tensor.matmul(bank[3][:, d * P:(d + 1) * P], W_sb[:, e, d * P:(d + 1) * P],
                                     exT[:, e, :], start=(e == 0), stop=(e == DK - 1))
            for e in range(DK):
                last = nc.tensor.matmul(bank[3][:, 2 * P:2 * P + 1], exT[:, e, :], col[:, 0, e:e + 1],
                                        start=(e == 0), stop=(e == DK - 1))
            last.then_inc(q_ps, 1)

            pe.wait_ge(ld_filt, 16)
            for o in range(ORDER):
                nc.tensor.matmul(bank[4 + o][:, 0:D], dft_s, filt[:, o, :], start=True, stop=True)
                nc.tensor.matmul(bank[4 + o][:, D:2 * D], dft_c, filt[:, o, :], start=True, stop=True
                                 ).then_inc(spec_ps, 1)
            pe.wait_ge(se_rdy, 1)
            for k in range(DK):
                for half in range(2):
                    n = 2 * k + half
                    b = (6, 7, 0, 1)[n]
                    for j in range(4):
                        last = nc.tensor.transpose(bank[b][:, j * P:(j + 1) * P],
                                                   se[:, 4 * half + j, k * P:(k + 1) * P], ident)
                    last.then_inc(seT_ps, 1)

            def transpose_ctx(loop, g, slot):
                pe.wait_ge(ld_raw[slot], raw_count(loop, g))
                for h in range(DK):
                    if g == 0:
                        pe.wait_ge(seT_rdy, 4)
                    else:
                        pe.wait_ge(cTlo_rdy, twice(loop, 2 * (g - 1) + h + 1))
                    for t in range(tiles_of(g) if loop is None else GT):
                        last = nc.tensor.transpose(bank[h][:, t * P:(t + 1) * P],
                                                   raw[:, slot, t, h * P:(h + 1) * P], ident)
                    last.then_inc(cT_ps, 1)

            def scores(loop, g, n):
                pe.wait_ge(cTlo_rdy, twice(loop, 2 * g + 2))
                if g == 0:
                    pe.wait_ge(q_rdy, 1)
                if g >= 2:
                    pe.wait_ge(prob_rdy, times(loop, g - 1))
                r = g % 2
                for h in range(DK):
                    nc.tensor.matmul(bank[2 + r][:, 0:n], q_hi[:, h, :], cT_hi[:, r, h, 0:n],
                                     start=(h == 0), stop=False)
                    nc.tensor.matmul(bank[2 + r][:, 0:n], q_hi[:, h, :], cT_lo[:, r, h, 0:n],
                                     start=False, stop=False)
                    last = nc.tensor.matmul(bank[2 + r][:, 0:n], q_lo[:, h, :], cT_hi[:, r, h, 0:n],
                                            start=False, stop=(h == DK - 1))
                last.then_inc(score_ps, 1)

            def transpose_prob(loop, g, nt):
                pe.wait_ge(prob_rdy, times(loop, g + 1))
                if g >= 2:
                    pe.wait_ge(pTlo_rdy, times(loop, g - 1))
                elif g == 0:
                    pe.wait_ge(spec_rdy, 6)
                for t in range(nt):
                    last = nc.tensor.transpose(bank[4 + g % 2][:, t * P:(t + 1) * P],
                                               prob[:, g % 2, t * P:(t + 1) * P], ident)
                last.then_inc(pT_ps, 1)

            def weigh(loop, g, slot, nt):
                pe.wait_ge(pTlo_rdy, times(loop, g + 1))
                pe.wait_ge(clo_rdy, times(loop, g + 1))
                if loop is not None or g >= 2:
                    pe.wait_ge(O_upd, times(loop, g))
                r = g % 2
                for t in range(nt):
                    ph, pl = pT_hi[:, r, t * P:(t + 1) * P], pT_lo[:, r, t * P:(t + 1) * P]
                    nc.tensor.matmul(bank[6 + r][:, 0:D], ph, c_hi[:, slot, t, :],
                                     start=(t == 0), stop=False)
                    nc.tensor.matmul(bank[6 + r][:, 0:D], ph, c_lo[:, slot, t, :],
                                     start=False, stop=False)
                    last = nc.tensor.matmul(bank[6 + r][:, 0:D], pl, c_hi[:, slot, t, :],
                                            start=False, stop=(t == nt - 1))
                last.then_inc(pv_ps, 1)

            def step(loop, i):
                if i + 1 < GROUPS:
                    transpose_ctx(loop, i + 1, (i + 1) % RING)
                if i < GROUPS:
                    scores(loop, i, GT * P if loop is not None else tiles_of(i) * P)
                if 1 <= i <= GROUPS:
                    transpose_prob(loop, i - 1, GT if loop is not None else tiles_of(i - 1))
                if i >= 2:
                    weigh(loop, i - 2, (i - 2) % RING, GT if loop is not None else tiles_of(i - 2))

            transpose_ctx(None, 0, 0)
            for i in range(FIRST):
                step(None, i)
            with pe.Fori(0, LOOPS) as n:
                for u in range(RING):
                    step(n, FIRST + u)
            for i in range(FIRST + RING * LOOPS, GROUPS + 2):
                step(None, i)

            transpose_xh(pe, 1)
            pe.wait_ge(xhT_rdy, 2)
            pe.wait_ge(ld_pw, 32)
            for lo, hi, b in ((0, D, 2), (D, 3 * D, 3)):
                for k in range(DK):
                    last = nc.tensor.matmul(bank[b][:, 0:hi - lo], xhT[:, k, :], pw[:, k, lo:hi],
                                            start=(k == 0), stop=(k == DK - 1))
                last.then_inc(proj_ps, 1)
            for o in range(ORDER):
                pe.wait_ge(v_rdy, o + 1)
                nc.tensor.matmul(bank[4][:, 0:D], dft_c, vbuf[:, o, :], start=True, stop=True)
                nc.tensor.matmul(bank[4][:, D:2 * D], dft_s, vbuf[:, o, :], start=True, stop=True
                                 ).then_inc(freq_ps, 1)
                for half, inv in ((0, inv_s), (1, inv_c)):
                    pe.wait_ge(prod_rdy, 2 * o + half + 1)
                    for part in range(2):
                        last = nc.tensor.matmul(bank[5][:, 0:D], inv, prod[:, half, part * D:(part + 1) * D],
                                                start=(half == 0 and part == 0),
                                                stop=(half == 1 and part == 1))
                last.then_inc(conv_ps, 1)

            pe.wait_ge(z_rdy, 1)
            for k in range(DK):
                last = nc.tensor.transpose(bank[1][:, k * P:(k + 1) * P], xh[:, k * P:(k + 1) * P], ident)
            last.then_inc(zT_ps, 1)
            pe.wait_ge(xnT_rdy, DK)
            for half in range(2):
                for j in range(4):
                    for k in range(DK):
                        last = nc.tensor.matmul(bank[2 + half][:, j * P:(j + 1) * P],
                                                seT[:, k, (4 * half + j) * P:(4 * half + j + 1) * P],
                                                xnT[:, k, :], start=(k == 0), stop=(k == DK - 1))
                last.then_inc(LT_ps, 1)
            for half in range(2):
                for k in range(DK):
                    last = nc.tensor.matmul(bank[6 + half][:, :], xnT[:, k, :],
                                            seT[:, k, half * 512:(half + 1) * 512],
                                            start=(k == 0), stop=(k == DK - 1))
                last.then_inc(L_ps, 1)
            for half in range(2):
                pe.wait_ge(dT_rdy, half + 1)
                for j in range(4):
                    last = nc.tensor.transpose(bank[4 + half][:, j * P:(j + 1) * P],
                                               dT[:, 4 * half + j, :], ident)
                last.then_inc(disp_ps, 1)
                pe.wait_ge(disp_rdy, half + 1)
                pe.wait_ge(xn_rdy, 1)
                for k in range(DK):
                    if half == 1:
                        pe.wait_ge(slots_rdy[k], 1)
                    nc.tensor.matmul(bank[k][:, :], xn[:, k * P:(k + 1) * P],
                                     disp[:, half * 512:(half + 1) * 512],
                                     start=True, stop=True).then_inc(slots_ps, 1)
            for half in range(2):
                pe.wait_ge(cexp_rdy, half + 1)
                for j in range(4):
                    last = nc.tensor.transpose(bank[2 + half][:, j * P:(j + 1) * P],
                                               comb[:, (4 * half + j) * P:(4 * half + j + 1) * P], ident)
                last.then_inc(combT_ps, 1)

            def hidden_of(p, which, b, done):
                s = p % WSLOTS
                pe.wait_ge(ld_wgu[s], 32 * (p // WSLOTS + 1))
                for k in range(DK):
                    for a in range(2):
                        last = nc.tensor.matmul(bank[b][a * SL:(a + 1) * SL, :],
                                                slotsT[:, k, p * P + a * SL:p * P + (a + 1) * SL],
                                                w_gu[s][:, which, a, k, :], start=(k == 0), stop=(k == DK - 1))
                last.then_inc(done, 1)

            def down_of(p):
                s = p % WSLOTS
                pe.wait_ge(hidT_rdy, p + 1)
                pe.wait_ge(ld_wd[s], 16 * (p // WSLOTS + 1))
                if p >= 1:
                    pe.wait_ge(eout_rdy, p)
                for c in range(FC):
                    for a in range(2):
                        last = nc.tensor.matmul(bank[5][a * SL:(a + 1) * SL, 0:D],
                                                hidT[:, c, a * SL:(a + 1) * SL], w_d[s][:, a, c, :],
                                                start=(c == 0), stop=(c == FC - 1))
                last.then_inc(down_ps, 1)

            def hidden_transpose(p):
                pe.wait_ge(hid_rdy, p + 1)
                if p >= 1:
                    pe.wait_ge(hidT_rdy, p)
                for c in range(FC):
                    last = nc.tensor.transpose(bank[4][:, c * P:(c + 1) * P], hid[:, c * P:(c + 1) * P], ident)
                last.then_inc(hidT_ps, 1)

            def mix_of(p):
                pe.wait_ge(eout_rdy, p + 1)
                last = nc.tensor.matmul(bank[6][:, 0:D], combT[:, p, :], eout[:, :],
                                        start=(p == 0), stop=(p == PAIRS - 1))
                last.then_inc(mix_ps, 1)

            for p in range(PAIRS + 1):
                if p < PAIRS:
                    if p == 0:
                        for k in range(DK):
                            pe.wait_ge(slots_rdy[k], 2)
                    elif p >= 2:
                        pe.wait_ge(gate_rdy, p - 1)
                    hidden_of(p, 0, p % 2, gate_ps)
                if p >= 1:
                    hidden_transpose(p - 1)
                if p < PAIRS:
                    if p == 0:
                        pe.wait_ge(combT_rdy, 2)
                    elif p >= 2:
                        pe.wait_ge(up_rdy, p - 1)
                    hidden_of(p, 1, 2 + p % 2, up_ps)
                if p >= 2:
                    mix_of(p - 2)
                if p >= 1:
                    down_of(p - 1)
            mix_of(PAIRS - 1)

        @block.scalar
        def _(act):
            act.dma_start(scale_b[:, :], scale.rearrange("(a n) -> a n", a=1).broadcast_to([P, 1])
                          ).then_inc(ld_scale, 16)
            act.dma_start(filt[:, :, :], filter_time[:, 0, 0:P, :].rearrange("o t d -> t o d")
                          ).then_inc(ld_filt, 16)
            act.wait_ge(WT_ps, 1)
            nc.scalar.activation(WT[:, :, :].rearrange("p k e -> p (k e)"), bank[0][:, :], ACT.Copy
                                 ).then_inc(WT_rdy, 1)
            act.wait_ge(q_ps, 1)
            nc.scalar.activation(q_hi[:, :, :].rearrange("p k q -> p (k q)"), bank[3][:, 0:D], ACT.Copy
                                 ).then_inc(qhi_rdy, 1)
            act.dma_start(pw[:, :, :], proj_w.rearrange("(k p) e -> p k e", p=P)).then_inc(ld_pw, 16)
            act.dma_start(pb[:, :], proj_b.rearrange("(a n) -> a n", a=1).broadcast_to([P, 3 * D])
                          ).then_inc(ld_pw, 16)
            for i, v in enumerate((norm_g, norm_b)):
                act.dma_start(g_row[:, i, :], v.rearrange("(a n) -> a n", a=1).broadcast_to([P, D])
                              ).then_inc(ld_row, 16)
            for o in range(ORDER):
                act.wait_ge(spec_ps, o + 1)
                nc.scalar.activation(spec[:, o, 0, :], bank[4 + o][:, 0:D], ACT.Copy).then_inc(spec_rdy, 1)
                nc.scalar.activation(spec[:, o, 1, :], bank[4 + o][:, D:2 * D], ACT.Copy).then_inc(spec_rdy, 1)
                nc.scalar.activation(spec[:, o, 2, :], bank[4 + o][:, 0:D], ACT.Copy, scale=-1.0
                                     ).then_inc(spec_rdy, 1)
            act.wait_ge(gs_rdy, 1)
            for n in range(4):
                act.wait_ge(seT_ps, n + 1)
                k, half = n // 2, n % 2
                nc.scalar.activation(seT[:, k, half * 512:(half + 1) * 512], bank[(6, 7, 0, 1)[n]][:, :],
                                     ACT.Identity, scale=col[:, 1, k:k + 1], bias=col[:, 2, k:k + 1]
                                     ).then_inc(seT_rdy, 1)
            for p in range(2):
                for i, w in enumerate((Wg, Wu)):
                    act.dma_start(w_gu[p][:, i, :, :, :].rearrange("p e k f -> p (e k) f"),
                                  w[2 * p:2 * p + 2, :, :].rearrange("e (k p) f -> p (e k) f", p=P)
                                  ).then_inc(ld_wgu[p], 16)
                act.dma_start(w_d[p][:, :, :, :].rearrange("p e c o -> p (e c) o"),
                              Wd[2 * p:2 * p + 2, :, :].rearrange("e (c p) o -> p (e c) o", p=P)
                              ).then_inc(ld_wd[p], 16)

            def ctx_hi(loop, g, n):
                for h in range(DK):
                    act.wait_ge(cT_ps, twice(loop, 2 * g + h + 1))
                    if g >= 2:
                        act.wait_ge(score_ps, times(loop, g - 1))
                    nc.scalar.activation(cT_hi[:, g % 2, h, 0:n], bank[h][:, 0:n], ACT.Copy
                                         ).then_inc(cThi_rdy, 1)

            def prob_hi(loop, g, n):
                act.wait_ge(pT_ps, times(loop, g + 1))
                if g >= 2:
                    act.wait_ge(pv_ps, times(loop, g - 1))
                nc.scalar.activation(pT_hi[:, g % 2, 0:n], bank[4 + g % 2][:, 0:n], ACT.Copy
                                     ).then_inc(pThi_rdy, 1)

            def exps(loop, g, n):
                act.wait_ge(ebias_rdy, times(loop, g + 1))
                if g >= 2:
                    act.wait_ge(pT_ps, times(loop, g - 1))
                nc.scalar.activation(prob[:, g % 2, 0:n], bank[2 + g % 2][:, 0:n], ACT.Exp,
                                     bias=ebias[:, g % RING:g % RING + 1],
                                     accum_out=rsum[:, g % RING:g % RING + 1]).then_inc(prob_rdy, 1)
                nc.scalar.activation(alpha[:, g % RING:g % RING + 1],
                                     negm[:, (g - 1) % RING:(g - 1) % RING + 1], ACT.Exp, scale=-1.0,
                                     bias=negm[:, g % RING:g % RING + 1]).then_inc(alpha_rdy, 1)

            def step(loop, i):
                full = loop is not None
                if i + 1 < GROUPS:
                    ctx_hi(loop, i + 1, (GT if full else tiles_of(i + 1)) * P)
                if 1 <= i <= GROUPS:
                    prob_hi(loop, i - 1, (GT if full else tiles_of(i - 1)) * P)
                if i < GROUPS:
                    exps(loop, i, (GT if full else tiles_of(i)) * P)

            ctx_hi(None, 0, GT * P)
            for i in range(FIRST):
                step(None, i)
            with act.Fori(0, LOOPS) as n:
                for u in range(RING):
                    step(n, FIRST + u)
            for i in range(FIRST + RING * LOOPS, GROUPS + 1):
                step(None, i)

            act.wait_ge(zT_ps, 1)
            for k in range(DK):
                nc.scalar.activation(xnT[:, k, :], bank[1][:, k * P:(k + 1) * P], ACT.Identity,
                                     scale=col[:, 3, k:k + 1], bias=col[:, 4, k:k + 1]
                                     ).then_inc(xnT_rdy, 1)
            for half in range(2):
                act.wait_ge(cmax_rdy, half + 1)
                for j in range(4):
                    c = 4 * half + j
                    last = nc.scalar.activation(dT[:, c, :], bank[2 + half][:, j * P:(j + 1) * P], ACT.Exp,
                                                bias=cmax[:, c:c + 1], accum_out=csum[:, c:c + 1])
                last.then_inc(dexp_rdy, 1)
            act.wait_ge(rmax_rdy, 1)
            for half in range(2):
                nc.scalar.activation(comb[:, half * 512:(half + 1) * 512], bank[6 + half][:, :], ACT.Exp,
                                     bias=rmax[:, 2:3], accum_out=rs[:, half:half + 1]).then_inc(cexp_rdy, 1)
            for half in range(2):
                act.wait_ge(slots_ps, 2 * half + 2)
                nc.scalar.activation(slotsT[:, 1, half * 512:(half + 1) * 512], bank[1][:, :], ACT.Copy
                                     ).then_inc(slots_rdy[1], 1)
            for half in range(2):
                act.wait_ge(combT_ps, half + 1)
                nc.scalar.activation(combT[:, 4 * half:4 * half + 4, :].rearrange("p j n -> p (j n)"),
                                     bank[2 + half][:, :], ACT.Copy).then_inc(combT_rdy, 1)
            for p in range(PAIRS):
                act.wait_ge(gate_rdy, p + 1)
                nc.scalar.activation(gate[:, p % 2, :], gate[:, p % 2, :], ACT.Gelu).then_inc(gelu_rdy, 1)
                act.wait_ge(hidT_ps, p + 1)
                if p >= 1:
                    act.wait_ge(down_ps, p)
                nc.scalar.activation(hidT[:, :, :].rearrange("p c s -> p (c s)"), bank[4][:, :], ACT.Copy
                                     ).then_inc(hidT_rdy, 1)

        @block.gpsimd
        def _(pool):
            nc.gpsimd.memset(neg_half[:, :], -0.5).then_inc(half_set, 1)
            nc.gpsimd.memset(zero[:, :], 0.0).then_inc(half_set, 1)
            pool.wait_ge(half_set, 2)

            def power(n, dst, src, width):
                pool.wait_ge(var_rdy, n + 1)
                nc.gpsimd.tensor_tensor(dst, src, neg_half[:, 0:width], ALU.pow).then_inc(rstd_rdy, 1)

            power(0, rstd[:, 0:1], mv[:, 1:2], 1)
            power(1, se_rstd[:, :], se_mv[:, :, 1], PAIRS)

            def split_ctx(loop, g, slot, nt):
                pool.wait_ge(ld_raw[slot], raw_count(loop, g))
                if g >= RING:
                    pool.wait_ge(pv_ps, times(loop, g - RING + 1))
                nc.gpsimd.tensor_tensor(c_hi[:, slot, 0:nt, :].rearrange("p t d -> p (t d)"),
                                        raw[:, slot, 0:nt, :].rearrange("p t d -> p (t d)"),
                                        zero[:, 0:1].broadcast_to([P, nt * D]), ALU.add).then_inc(chi_rdy, 1)
                pool.wait_ge(chi_rdy, times(loop, g + 1))
                nc.gpsimd.tensor_tensor(c_lo[:, slot, 0:nt, :], raw[:, slot, 0:nt, :],
                                        c_hi[:, slot, 0:nt, :].bitcast(fp32), ALU.subtract
                                        ).then_inc(clo_rdy, 1)

            pool.wait_ge(q_ps, 1)
            pool.wait_ge(seT_ps, 4)
            for g in range(RING):
                split_ctx(None, g, g, GT)
            with pool.Fori(0, LOOPS) as n:
                for u in range(RING):
                    split_ctx(n, RING + u, u, GT)
            split_ctx(None, LAST, LAST % RING, LAST_T)
            for n in range(2, 5):
                power(n, rstd[:, 0:1], mv[:, 1:2], 1)
            for p in range(PAIRS):
                if p >= 2:
                    pool.wait_ge(eout_rdy, p - 1)
                load_bias(pool, p)

        @block.vector
        def _(dve):
            count = [0]

            def link(ins):
                count[0] += 1
                ins.then_inc(dve_n, 1)
                dve.wait_ge(dve_n, count[0])

            def norm(n, src, dst, done):
                link(nc.vector.bn_stats(stat6[:, :], src))
                link(nc.vector.bn_aggr(mv[:, :], stat6[:, :]))
                nc.vector.tensor_scalar(mv[:, 1:2], mv[:, 1:2], EPS, None, ALU.add).then_inc(var_rdy, 1)
                dve.wait_ge(rstd_rdy, n + 1)
                last = nc.vector.tensor_scalar(dst, src, mv[:, 0:1], rstd[:, 0:1], ALU.subtract, ALU.mult)
                if done is None:
                    link(last)
                else:
                    last.then_inc(done, 1)

            dve.wait_ge(ld_x, 16)
            norm(0, x_sb[:, :], xh[:, :], xh_rdy)
            dve.wait_ge(xhT_ps, 1)
            nc.vector.tensor_copy(xhT[:, :, :].rearrange("p k t -> p (k t)"), bank[1][:, 0:D]).then_inc(xhT_rdy, 1)
            dve.wait_ge(ld_col, 16)
            dve.wait_ge(exT_ps, 1)
            for e in range(DK):
                last = nc.vector.tensor_scalar(exT[:, e, :], bank[2][:, e * P:(e + 1) * P], col[:, 0, e:e + 1],
                                               None, ALU.add)
            last.then_inc(exT_rdy, 1)
            dve.wait_ge(qhi_rdy, 1)
            nc.vector.tensor_tensor(q_lo[:, :, :].rearrange("p k q -> p (k q)"), bank[3][:, 0:D],
                                    q_hi[:, :, :].rearrange("p k q -> p (k q)").bitcast(fp32), ALU.subtract
                                    ).then_inc(q_rdy, 1)
            nc.vector.tensor_copy(s0[:, :], bank[3][:, 2 * P:2 * P + 1]).then_inc(s0_rdy, 1)
            nc.vector.memset(negm[:, RING - 1:RING], BIG)
            nc.vector.memset(lsum[:, :], 0.0)
            nc.vector.memset(O[:, :], 0.0).then_inc(O_upd, 1)
            dve.wait_ge(ld_scale, 16)
            for i in (1, 2):
                last = nc.vector.tensor_scalar(col[:, i, :], col[:, i, :], scale_b[:, 0:1], None, ALU.mult)
            last.then_inc(gs_rdy, 1)
            dve.wait_ge(ld_se, 16)
            for j in range(PAIRS):
                last = nc.vector.bn_stats(se_stat[:, j, :], se[:, j, :])
            link(last)
            for j in range(PAIRS):
                last = nc.vector.bn_aggr(se_mv[:, j, :], se_stat[:, j, :])
            link(last)
            nc.vector.tensor_scalar(se_mv[:, :, 1], se_mv[:, :, 1], EPS, None, ALU.add).then_inc(var_rdy, 1)
            dve.wait_ge(rstd_rdy, 2)
            for j in range(PAIRS):
                last = nc.vector.tensor_scalar(se[:, j, :], se[:, j, :], se_mv[:, j, 0:1], se_rstd[:, j:j + 1],
                                               ALU.subtract, ALU.mult)
            last.then_inc(se_rdy, 1)

            def ctx_lo(loop, g, n):
                for h in range(DK):
                    dve.wait_ge(cThi_rdy, twice(loop, 2 * g + h + 1))
                    nc.vector.tensor_tensor(cT_lo[:, g % 2, h, 0:n], bank[h][:, 0:n],
                                            cT_hi[:, g % 2, h, 0:n].bitcast(fp32), ALU.subtract
                                            ).then_inc(cTlo_rdy, 1)

            def running_max(loop, g, n):
                r = g % RING
                dve.wait_ge(score_ps, times(loop, g + 1))
                nc.vector.tensor_reduce(gmax[:, :], bank[2 + g % 2][:, 0:n], AX.X, ALU.max, negate=True
                                        ).then_inc(gmax_rdy, 1)
                dve.wait_ge(gmax_rdy, times(loop, g + 1))
                nc.vector.scalar_tensor_tensor(out=negm[:, r:r + 1], in0=gmax[:, :], scalar=s0[:, 0:1],
                                               in1=negm[:, (g - 1) % RING:(g - 1) % RING + 1],
                                               op0=ALU.subtract, op1=ALU.min).then_inc(negm_rdy, 1)
                dve.wait_ge(negm_rdy, times(loop, g + 1))
                nc.vector.tensor_tensor(ebias[:, r:r + 1], negm[:, r:r + 1], s0[:, :], ALU.add
                                        ).then_inc(ebias_rdy, 1)

            def prob_lo(loop, g, n):
                dve.wait_ge(pThi_rdy, times(loop, g + 1))
                nc.vector.tensor_tensor(pT_lo[:, g % 2, 0:n], bank[4 + g % 2][:, 0:n],
                                        pT_hi[:, g % 2, 0:n].bitcast(fp32), ALU.subtract).then_inc(pTlo_rdy, 1)

            def update(loop, g):
                r = g % RING
                dve.wait_ge(alpha_rdy, times(loop, g + 1))
                if g >= 1:
                    dve.wait_ge(l_upd, times(loop, g))
                nc.vector.scalar_tensor_tensor(out=lsum[:, :], in0=lsum[:, :], scalar=alpha[:, r:r + 1],
                                               in1=rsum[:, r:r + 1], op0=ALU.mult, op1=ALU.add).then_inc(l_upd, 1)
                dve.wait_ge(pv_ps, times(loop, g + 1))
                dve.wait_ge(O_upd, times(loop, g + 1))
                nc.vector.scalar_tensor_tensor(out=O[:, :], in0=O[:, :], scalar=alpha[:, r:r + 1],
                                               in1=bank[6 + g % 2][:, 0:D], op0=ALU.mult, op1=ALU.add
                                               ).then_inc(O_upd, 1)

            def step(loop, i):
                full = loop is not None
                if i + 1 < GROUPS:
                    ctx_lo(loop, i + 1, (GT if full else tiles_of(i + 1)) * P)
                if i < GROUPS:
                    running_max(loop, i, (GT if full else tiles_of(i)) * P)
                if 1 <= i <= GROUPS:
                    prob_lo(loop, i - 1, (GT if full else tiles_of(i - 1)) * P)
                if i >= 2:
                    update(loop, i - 2)

            dve.wait_ge(s0_rdy, 1)
            ctx_lo(None, 0, GT * P)
            for i in range(FIRST):
                step(None, i)
            with dve.Fori(0, LOOPS) as n:
                for u in range(RING):
                    step(n, FIRST + u)
            for i in range(FIRST + RING * LOOPS, GROUPS + 2):
                step(None, i)

            dve.wait_ge(l_upd, GROUPS)
            dve.wait_ge(O_upd, GROUPS + 1)
            link(nc.vector.reciprocal(linv[:, :], lsum[:, :]))
            link(nc.vector.scalar_tensor_tensor(out=x1[:, :], in0=O[:, :], scalar=linv[:, 0:1], in1=x_sb[:, :],
                                                op0=ALU.mult, op1=ALU.add))
            norm(2, x1[:, :], xh[:, :], xh_rdy)
            dve.wait_ge(xhT_ps, 2)
            nc.vector.tensor_copy(xhT[:, :, :].rearrange("p k t -> p (k t)"), bank[1][:, 0:D]).then_inc(xhT_rdy, 1)
            dve.wait_ge(ld_pw, 32)
            dve.wait_ge(proj_ps, 1)
            nc.vector.tensor_tensor(vbuf[:, 0, :], bank[2][:, 0:D], pb[:, 0:D], ALU.add).then_inc(v_rdy, 1)
            dve.wait_ge(proj_ps, 2)
            link(nc.vector.tensor_tensor(p_sb[:, D:3 * D], bank[3][:, :], pb[:, D:3 * D], ALU.add))
            for o in range(ORDER):
                dve.wait_ge(freq_ps, o + 1)
                for half in range(2):
                    nc.vector.tensor_tensor(prod[:, half, :], bank[4][:, :],
                                            spec[:, o, half:half + 2, :].rearrange("p a d -> p (a d)"), ALU.mult
                                            ).then_inc(prod_rdy, 1)
                dve.wait_ge(conv_ps, o + 1)
                if o + 1 < ORDER:
                    nc.vector.tensor_tensor(vbuf[:, o + 1, :], bank[5][:, 0:D], p_sb[:, (o + 1) * D:(o + 2) * D],
                                            ALU.mult).then_inc(v_rdy, 1)
                else:
                    link(nc.vector.tensor_tensor(xn[:, :], bank[5][:, 0:D], p_sb[:, (o + 1) * D:(o + 2) * D],
                                                 ALU.mult))
            link(nc.vector.tensor_tensor(x2[:, :], x1[:, :], xn[:, :], ALU.add))
            norm(3, x2[:, :], xn[:, :], None)
            norm(4, xn[:, :], xh[:, :], z_rdy)
            dve.wait_ge(ld_row, 32)
            dve.wait_ge(z_rdy, 1)
            link(nc.vector.tensor_tensor(xn[:, :], xh[:, :], g_row[:, 0, :], ALU.mult))
            nc.vector.tensor_tensor(xn[:, :], xn[:, :], g_row[:, 1, :], ALU.add).then_inc(xn_rdy, 1)
            for half in range(2):
                dve.wait_ge(LT_ps, half + 1)
                nc.vector.tensor_reduce(cmax[:, 4 * half:4 * half + 4],
                                        bank[2 + half][:, :].rearrange("p (j n) -> p j n", n=P), AX.X, ALU.max,
                                        negate=True).then_inc(cmax_rdy, 1)
            for half in range(2):
                hs = slice(4 * half, 4 * half + 4)
                dve.wait_ge(dexp_rdy, half + 1)
                link(nc.vector.reciprocal(cinv[:, hs], csum[:, hs]))
                nc.vector.tensor_tensor(dT[:, hs, :], dT[:, hs, :],
                                        cinv[:, hs].unsqueeze(2).broadcast_to([P, 4, P]), ALU.mult
                                        ).then_inc(dT_rdy, 1)
                if half == 0:
                    for q in range(2):
                        dve.wait_ge(L_ps, q + 1)
                        last = nc.vector.tensor_reduce(rmax[:, q:q + 1], bank[6 + q][:, :], AX.X, ALU.max,
                                                       negate=True)
                    link(last)
                    nc.vector.tensor_tensor(rmax[:, 2:3], rmax[:, 0:1], rmax[:, 1:2], ALU.min
                                            ).then_inc(rmax_rdy, 1)
                dve.wait_ge(disp_ps, half + 1)
                nc.vector.tensor_copy(disp[:, half * 512:(half + 1) * 512], bank[4 + half][:, :]
                                      ).then_inc(disp_rdy, 1)
                dve.wait_ge(slots_ps, 2 * half + 1)
                nc.vector.tensor_copy(slotsT[:, 0, half * 512:(half + 1) * 512], bank[0][:, :]
                                      ).then_inc(slots_rdy[0], 1)
            dve.wait_ge(cexp_rdy, 2)
            link(nc.vector.tensor_tensor(rs[:, 2:3], rs[:, 0:1], rs[:, 1:2], ALU.add))
            link(nc.vector.reciprocal(rs[:, 3:4], rs[:, 2:3]))
            for p in range(PAIRS + 1):
                if p < PAIRS:
                    dve.wait_ge(ld_bias[p % 2], BIAS_LOADS * (p // 2 + 1))
                    dve.wait_ge(gate_ps, p + 1)
                    if p >= 2:
                        dve.wait_ge(hid_rdy, p - 1)
                    nc.vector.tensor_tensor(gate[:, p % 2, :], bank[p % 2][:, :], bias_gu[:, p % 2, 0, :], ALU.add
                                            ).then_inc(gate_rdy, 1)
                    dve.wait_ge(up_ps, p + 1)
                    if p >= 1:
                        dve.wait_ge(hid_rdy, p)
                    nc.vector.tensor_tensor(up[:, :], bank[2 + p % 2][:, :], bias_gu[:, p % 2, 1, :], ALU.add
                                            ).then_inc(up_rdy, 1)
                    dve.wait_ge(up_rdy, p + 1)
                    dve.wait_ge(gelu_rdy, p + 1)
                    if p >= 1:
                        dve.wait_ge(hidT_ps, p)
                    nc.vector.tensor_tensor(hid[:, :], gate[:, p % 2, :], up[:, :], ALU.mult).then_inc(hid_rdy, 1)
                if p >= 1:
                    dve.wait_ge(down_ps, p)
                    if p >= 2:
                        dve.wait_ge(mix_ps, p - 1)
                    nc.vector.tensor_tensor(eout[:, :], bank[5][:, 0:D], bias_d[:, (p - 1) % 2, :], ALU.add
                                            ).then_inc(eout_rdy, 1)
            dve.wait_ge(mix_ps, PAIRS)
            nc.vector.scalar_tensor_tensor(out=x1[:, :], in0=bank[6][:, 0:D], scalar=rs[:, 3:4], in1=x2[:, :],
                                           op0=ALU.mult, op1=ALU.add).then_inc(res_rdy, 1)


def spectrum_tables(np, n):
    t = np.arange(n)[:, None]
    w = 2.0 * np.pi * (np.arange(n)[None, :] + 0.5) / (2 * n)
    c, s = np.cos(t * w), np.sin(t * w)
    return np.stack([np.eye(n), c, s, c.T / n, s.T / n], axis=1).astype(np.float32)


_INS = ['x', 'ctx_1024', 'L0_xattn_W', 'L0_xattn_b', 'L0_attn_proj_w', 'L0_attn_proj_b', 'L0_attn_filter_time',
        'L0_ffn_norm_g', 'L0_ffn_norm_b', 'L0_ffn_slot_g', 'L0_ffn_slot_b', 'L0_ffn_scale', 'L0_ffn_slot_embeds',
        'L0_ffn_Wg', 'L0_ffn_bg', 'L0_ffn_Wu', 'L0_ffn_bu', 'L0_ffn_Wd', 'L0_ffn_bd']


def kernel(**inputs):
    import numpy as _np
    import concourse.bacc as _bacc
    from concourse import mybir as _mybir
    from concourse.bass_utils import run_bass_kernel_spmd as _run

    nc = _bacc.Bacc("TRN2", target_bir_lowering=False, num_devices=1)
    arrays, args = {}, []

    def add(name, a):
        arrays[name] = a
        args.append(nc.dram_tensor(name, a.shape, _mybir.dt.from_np(a.dtype), kind="ExternalInput").ap())

    for name in _INS:
        add(f"in_{name}_dram", _np.ascontiguousarray(inputs[name]))
    vectors = [inputs[n] for n in ('L0_xattn_b', 'L0_ffn_slot_g', 'L0_ffn_slot_b', 'L0_ffn_norm_g', 'L0_ffn_norm_b')]
    add("columns_dram", _np.ascontiguousarray(_np.stack(
        [_np.asarray(v).reshape(2, 128).transpose(1, 0) for v in vectors], axis=1)))
    add("tables_dram", spectrum_tables(_np, 128))
    args.append(nc.dram_tensor("out_0_dram", (1, 128, 256), _mybir.dt.from_np(_np.dtype("float32")),
                               kind="ExternalOutput").ap())
    perceiver_kernel(nc, *args)
    return _run(nc, [arrays], core_ids=[0]).results[0]["out_0_dram"]
```

```python
import concourse.bass as bass
from concourse import mybir
from contextlib import ExitStack


def perceiver_kernel(nc, x, ctx_in, xattn_W, proj_w, proj_b, filter_time, norm_g, norm_b,
                     scale, slot_embeds, Wg, Wu, Wd, biases, columns, tables, out):
    fp32 = mybir.dt.float32
    fp32r = mybir.dt.float32r
    ALU = mybir.AluOpType
    ACT = mybir.ActivationFunctionType
    AX = mybir.AxisListType

    P = 128
    D = x.shape[2]
    DK = D // P
    KEYS = ctx_in.shape[1]
    TILES = KEYS // P
    GT = 4
    GROUPS = -(-TILES // GT)
    LAST = GROUPS - 1
    LAST_T = TILES - LAST * GT
    RING = 4
    LOOPS = (GROUPS - 5) // RING
    FIRST = 3
    ORDER = filter_time.shape[0]
    E, SL = slot_embeds.shape[0], slot_embeds.shape[1]
    F = Wg.shape[2]
    FC = F // P
    PAIRS = E * SL // P
    SLOTS = E * SL
    WSLOTS = 5
    BSLOTS = 3
    EPS = 1e-5
    BIG = 3.0e38

    def tiles_of(g):
        return LAST_T if g == LAST else GT

    st = ExitStack()
    with st:
        def sem(name):
            return st.enter_context(nc.semaphore(name))

        def sb(name, shape, dt=fp32, where=st):
            return where.enter_context(nc.sbuf_tensor(name, shape, dt))

        bank = [st.enter_context(nc.psum_tensor(f"bank{i}", [P, 512], fp32)) for i in range(8)]

        tab = sb("tab", [P, 5, P])
        ident, dft_c, dft_s, inv_c, inv_s = (tab[:, i, :] for i in range(5))
        x_sb = sb("x_sb", [P, D])
        x1 = sb("x1", [P, D])
        x2 = sb("x2", [P, D])
        xh = sb("xh", [P, D])
        xhT = sb("xhT", [P, DK, P])
        xn = sb("xn", [P, D])
        xnT = sb("xnT", [P, DK, P])
        stat6 = sb("stat6", [P, 6])
        mv = sb("mv", [P, 2])
        rstd = sb("rstd", [P, 1])
        neg_half = sb("neg_half", [P, PAIRS])
        zero = sb("zero", [P, 1])
        col = sb("col", [P, 5, DK])
        scale_b = sb("scale_b", [P, 1])
        g_row = sb("g_row", [P, 2, D])
        pw = sb("pw", [P, DK, 3 * D])
        pb = sb("pb", [P, 3 * D])
        filt = sb("filt", [P, ORDER, D])
        spec = sb("spec", [P, ORDER, 3, D])
        seT = sb("seT", [P, DK, SLOTS])
        negm = sb("negm", [P, RING])
        ebias = sb("ebias", [P, RING])
        gmax = sb("gmax", [P, 1])
        rsum = sb("rsum", [P, RING])
        alpha = sb("alpha", [P, RING])
        s0 = sb("s0", [P, 1])
        lsum = sb("lsum", [P, 1])
        linv = sb("linv", [P, 1])
        O = sb("O", [P, D])
        slots_or_se = sb("slots_or_se", [P, DK * SLOTS])
        se = slots_or_se[:, :].rearrange("p (j d) -> p j d", d=D)
        slotsT = slots_or_se[:, :].rearrange("p (k s) -> p k s", k=DK)
        se_stat = sb("se_stat", [P, PAIRS, 6])
        se_mv = sb("se_mv", [P, PAIRS, 2])
        se_rstd = sb("se_rstd", [P, PAIRS])
        w_gu = [sb(f"w_gu{i}", [P, 2, 2, DK, F]) for i in range(2)]
        w_d = [sb(f"w_d{i}", [P, 2, FC, D]) for i in range(2)]
        bias = sb("bias", [P, BSLOTS, 2 * F + D])

        att = ExitStack()
        prob = sb("prob", [P, 2, GT * P], fp32, att)
        pT_hi = sb("pT_hi", [P, 2, GT * P], fp32r, att)
        pT_lo = sb("pT_lo", [P, 2, GT * P], fp32r, att)
        q_hi = sb("q_hi", [P, DK, P], fp32r, att)
        q_lo = sb("q_lo", [P, DK, P], fp32r, att)
        raw = sb("raw", [P, RING, GT, D], fp32, att)
        c_hi = sb("c_hi", [P, RING, GT, D], fp32r, att)
        c_lo = sb("c_lo", [P, RING, GT, D], fp32r, att)
        cT_hi = sb("cT_hi", [P, 2, DK, GT * P], fp32r, att)
        cT_lo = sb("cT_lo", [P, 2, DK, GT * P], fp32r, att)
        att.close()
        pre = ExitStack()
        W_sb = sb("W_sb", [P, DK, D], fp32, pre)
        WT = sb("WT", [P, DK, D], fp32, pre)
        exT = sb("exT", [P, DK, P], fp32, pre)
        pre.close()
        ffn = ExitStack()
        for i in range(2, WSLOTS):
            w_gu.append(sb(f"w_gu{i}", [P, 2, 2, DK, F], fp32, ffn))
            w_d.append(sb(f"w_d{i}", [P, 2, FC, D], fp32, ffn))
        dT = sb("dT", [P, PAIRS, P], fp32, ffn)
        combT = dT
        disp = sb("disp", [P, SLOTS], fp32, ffn)
        comb = sb("comb", [P, SLOTS], fp32, ffn)
        cmax = sb("cmax", [P, PAIRS], fp32, ffn)
        csum = sb("csum", [P, PAIRS], fp32, ffn)
        cinv = sb("cinv", [P, PAIRS], fp32, ffn)
        rmax = sb("rmax", [P, 1], fp32, ffn)
        rs = sb("rs", [P, 4], fp32, ffn)
        conv = ExitStack()
        p_sb = sb("p_sb", [P, 3 * D], fp32, conv)
        vbuf = sb("vbuf", [P, 2, D], fp32, conv)
        prod = sb("prod", [P, 2, 2 * D], fp32, conv)
        conv.close()
        gate = sb("gate", [P, 2, F], fp32, ffn)
        up = sb("up", [P, F], fp32, ffn)
        hid = sb("hid", [P, F], fp32, ffn)
        hidT = sb("hidT", [P, FC, P], fp32, ffn)
        eout = sb("eout", [P, D], fp32, ffn)
        ffn.close()

        ld_x, ld_W, ld_tab, ld_scale = sem("ld_x"), sem("ld_W"), sem("ld_tab"), sem("ld_scale")
        ld_se, ld_col, ld_row, ld_filt = sem("ld_se"), sem("ld_col"), sem("ld_row"), sem("ld_filt")
        ld_pw = sem("ld_pw")
        ld_raw = [sem(f"ld_raw{i}") for i in range(RING)]
        ld_wgu = [sem(f"ld_wgu{i}") for i in range(WSLOTS)]
        ld_wd = [sem(f"ld_wd{i}") for i in range(WSLOTS)]
        ld_bias = [sem(f"ld_bias{i}") for i in range(BSLOTS)]
        st_out = sem("st_out")
        dve_n = sem("dve_n")
        half_set = sem("half_set")
        var_rdy, rstd_rdy = sem("var_rdy"), sem("rstd_rdy")
        xh_rdy, xhT_ps, xhT_rdy = sem("xh_rdy"), sem("xhT_ps"), sem("xhT_rdy")
        WT_ps, WT_rdy = sem("WT_ps"), sem("WT_rdy")
        exT_ps, exT_rdy = sem("exT_ps"), sem("exT_rdy")
        q_ps, qhi_rdy, q_rdy, s0_rdy = sem("q_ps"), sem("qhi_rdy"), sem("q_rdy"), sem("s0_rdy")
        se_rdy, seT_ps, seT_rdy = sem("se_rdy"), sem("seT_ps"), sem("seT_rdy")
        gs_rdy = sem("gs_rdy")
        spec_ps, spec_rdy = sem("spec_ps"), sem("spec_rdy")
        cT_ps, cThi_rdy, cTlo_rdy = sem("cT_ps"), sem("cThi_rdy"), sem("cTlo_rdy")
        score_ps, gmax_rdy, negm_rdy, ebias_rdy = (sem("score_ps"), sem("gmax_rdy"), sem("negm_rdy"),
                                                   sem("ebias_rdy"))
        prob_rdy, alpha_rdy = sem("prob_rdy"), sem("alpha_rdy")
        pT_ps, pThi_rdy, pTlo_rdy = sem("pT_ps"), sem("pThi_rdy"), sem("pTlo_rdy")
        chi_rdy, chi2_rdy, clo_rdy = sem("chi_rdy"), sem("chi2_rdy"), sem("clo_rdy")
        pv_ps, O_upd, l_upd = sem("pv_ps"), sem("O_upd"), sem("l_upd")
        proj_ps, v_rdy, freq_ps = sem("proj_ps"), sem("v_rdy"), sem("freq_ps")
        prod_rdy, conv_ps = sem("prod_rdy"), sem("conv_ps")
        x2_rdy, z_rdy, zT_ps, xn_rdy, xnT_rdy = (sem("x2_rdy"), sem("z_rdy"), sem("zT_ps"),
                                                 sem("xn_rdy"), sem("xnT_rdy"))
        L_ps, L0_rdy, L1_rdy, LT_ps = sem("L_ps"), sem("L0_rdy"), sem("L1_rdy"), sem("LT_ps")
        cmax_rdy, dexp_rdy, dT_rdy = sem("cmax_rdy"), sem("dexp_rdy"), sem("dT_rdy")
        disp_ps, disp_rdy = sem("disp_ps"), sem("disp_rdy")
        slots_ps, slots_rdy = sem("slots_ps"), [sem(f"slots_rdy{k}") for k in range(DK)]
        rmax_rdy, cexp_rdy = sem("rmax_rdy"), sem("cexp_rdy")
        combT_ps, combT_rdy = sem("combT_ps"), sem("combT_rdy")
        gate_ps, up_ps, gate_rdy, up_rdy = sem("gate_ps"), sem("up_ps"), sem("gate_rdy"), sem("up_rdy")
        gelu_rdy, hid_rdy, hidT_ps, hidT_rdy = (sem("gelu_rdy"), sem("hid_rdy"), sem("hidT_ps"),
                                                sem("hidT_rdy"))
        down_ps, eout_rdy, mix_ps, res_rdy = sem("down_ps"), sem("eout_rdy"), sem("mix_ps"), sem("res_rdy")

        ctx_v = ctx_in[0, :, :].rearrange("(p j) d -> p j d", p=P)

        def times(loop, static):
            return static if loop is None else loop * RING + static

        def twice(loop, static):
            return static if loop is None else loop * (2 * RING) + static

        def raw_count(loop, g):
            n = 16 * (g // RING + 1)
            return n if loop is None else loop * 16 + n

        def load_bias(eng, p):
            s = p % BSLOTS
            for a in range(2):
                eng.dma_start(bias[a * SL:(a + 1) * SL, s, :],
                              biases[2 * p + a:2 * p + a + 1, :].broadcast_to([SL, 2 * F + D])
                              ).then_inc(ld_bias[s], 16)

        def load_hidden(eng, p):
            for i, w in enumerate((Wg, Wu)):
                eng.dma_start(w_gu[p % WSLOTS][:, i, :, :, :].rearrange("p e k f -> p (e k) f"),
                              w[2 * p:2 * p + 2, :, :].rearrange("e (k p) f -> p (e k) f", p=P)
                              ).then_inc(ld_wgu[p % WSLOTS], 16)

        def load_down(eng, p):
            eng.dma_start(w_d[p % WSLOTS][:, :, :, :].rearrange("p e c o -> p (e c) o"),
                          Wd[2 * p:2 * p + 2, :, :].rearrange("e (c p) o -> p (e c) o", p=P)
                          ).then_inc(ld_wd[p % WSLOTS], 16)

        def transpose_xh(pe, n):
            pe.wait_ge(xh_rdy, n + 1)
            for k in range(DK):
                last = nc.tensor.transpose(bank[1][:, k * P:(k + 1) * P], xh[:, k * P:(k + 1) * P], ident)
            last.then_inc(xhT_ps, 1)

        block = st.enter_context(nc.Block())

        @block.sync
        def _(sp):
            sp.dma_start(x_sb[:, :], x[0, :, :]).then_inc(ld_x, 16)
            sp.dma_start(tab[:, :, :], tables).then_inc(ld_tab, 16)
            sp.dma_start(W_sb[:, :, :], xattn_W.rearrange("(k p) d -> p k d", p=P)).then_inc(ld_W, 16)
            sp.dma_start(col[:, :, :], columns).then_inc(ld_col, 16)
            for g in range(RING):
                sp.dma_start(raw[:, g, :, :], ctx_v[:, g * GT:(g + 1) * GT, :]).then_inc(ld_raw[g], 16)
            with sp.Fori(0, LOOPS) as n:
                for u in range(RING):
                    sp.wait_ge(score_ps, n * RING + (u + 1))
                    sp.wait_ge(clo_rdy, n * RING + (u + 1))
                    sp.dma_start(raw[:, u, :, :], ctx_v[:, bass.ds(n * (RING * GT) + (RING + u) * GT, GT), :]
                                 ).then_inc(ld_raw[u], 16)
            u = LAST % RING
            sp.wait_ge(score_ps, LAST - RING + 1)
            sp.wait_ge(clo_rdy, LAST - RING + 1)
            sp.dma_start(raw[:, u, 0:LAST_T, :], ctx_v[:, LAST * GT:TILES, :]).then_inc(ld_raw[u], 16)
            sp.wait_ge(pv_ps, GROUPS)
            for p in range(2, WSLOTS):
                load_hidden(sp, p)
                load_down(sp, p)
            for p in range(WSLOTS, PAIRS):
                sp.wait_ge(up_ps, p - WSLOTS + 1)
                load_hidden(sp, p)
                sp.wait_ge(down_ps, p - WSLOTS + 1)
                load_down(sp, p)
            sp.wait_ge(res_rdy, 1)
            sp.dma_start(out[0, :, :], x1[:, :]).then_inc(st_out, 16)
            sp.wait_ge(st_out, 16)

        SE_BANK = (6, 7, 0, 2)

        @block.tensor
        def _(pe):
            pe.wait_ge(ld_tab, 16)
            pe.wait_ge(ld_W, 16)
            for d in range(DK):
                for e in range(DK):
                    last = nc.tensor.transpose(bank[0][:, (2 * d + e) * P:(2 * d + e + 1) * P],
                                               W_sb[:, e, d * P:(d + 1) * P], ident)
            last.then_inc(WT_ps, 1)
            transpose_xh(pe, 0)

            def spectrum(o):
                pe.wait_ge(ld_filt, 16)
                nc.tensor.matmul(bank[4 + o][:, 0:D], dft_s, filt[:, o, :], start=True, stop=True)
                nc.tensor.matmul(bank[4 + o][:, D:2 * D], dft_c, filt[:, o, :], start=True, stop=True
                                 ).then_inc(spec_ps, 1)

            pe.wait_ge(WT_rdy, 1)
            pe.wait_ge(xhT_rdy, 1)
            for e in range(DK):
                for d in range(DK):
                    last = nc.tensor.matmul(bank[2][:, e * P:(e + 1) * P], WT[:, d, e * P:(e + 1) * P],
                                            xhT[:, d, :], start=(d == 0), stop=(d == DK - 1))
            last.then_inc(exT_ps, 1)
            spectrum(0)
            pe.wait_ge(exT_rdy, 1)
            for d in range(DK):
                for e in range(DK):
                    nc.tensor.matmul(bank[3][:, d * P:(d + 1) * P], W_sb[:, e, d * P:(d + 1) * P],
                                     exT[:, e, :], start=(e == 0), stop=(e == DK - 1))
            for e in range(DK):
                last = nc.tensor.matmul(bank[3][:, 2 * P:2 * P + 1], exT[:, e, :], col[:, 0, e:e + 1],
                                        start=(e == 0), stop=(e == DK - 1))
            last.then_inc(q_ps, 1)

            def transpose_ctx(loop, g, slot):
                pe.wait_ge(ld_raw[slot], raw_count(loop, g))
                for h in range(DK):
                    if loop is not None or g >= 1:
                        pe.wait_ge(cTlo_rdy, twice(loop, 2 * (g - 1) + h + 1))
                    for t in range(tiles_of(g) if loop is None else GT):
                        last = nc.tensor.transpose(bank[h][:, t * P:(t + 1) * P],
                                                   raw[:, slot, t, h * P:(h + 1) * P], ident)
                    last.then_inc(cT_ps, 1)

            def scores(loop, g, n):
                pe.wait_ge(cTlo_rdy, twice(loop, 2 * g + 2))
                if g == 0:
                    pe.wait_ge(q_rdy, 1)
                if g >= 2:
                    pe.wait_ge(prob_rdy, times(loop, g - 1))
                r = g % 2
                for h in range(DK):
                    nc.tensor.matmul(bank[2 + r][:, 0:n], q_hi[:, h, :], cT_hi[:, r, h, 0:n],
                                     start=(h == 0), stop=False)
                    nc.tensor.matmul(bank[2 + r][:, 0:n], q_hi[:, h, :], cT_lo[:, r, h, 0:n],
                                     start=False, stop=False)
                    last = nc.tensor.matmul(bank[2 + r][:, 0:n], q_lo[:, h, :], cT_hi[:, r, h, 0:n],
                                            start=False, stop=(h == DK - 1))
                last.then_inc(score_ps, 1)

            def transpose_prob(loop, g, nt):
                pe.wait_ge(prob_rdy, times(loop, g + 1))
                if g >= 2:
                    pe.wait_ge(pTlo_rdy, times(loop, g - 1))
                elif g == 0:
                    pe.wait_ge(spec_rdy, 4)
                for t in range(nt):
                    last = nc.tensor.transpose(bank[4 + g % 2][:, t * P:(t + 1) * P],
                                               prob[:, g % 2, t * P:(t + 1) * P], ident)
                last.then_inc(pT_ps, 1)

            def weigh(loop, g, slot, nt):
                pe.wait_ge(pTlo_rdy, times(loop, g + 1))
                pe.wait_ge(clo_rdy, times(loop, g + 1))
                if loop is not None or g >= 2:
                    pe.wait_ge(O_upd, times(loop, g))
                r = g % 2
                for t in range(nt):
                    ph, pl = pT_hi[:, r, t * P:(t + 1) * P], pT_lo[:, r, t * P:(t + 1) * P]
                    nc.tensor.matmul(bank[6 + r][:, 0:D], ph, c_hi[:, slot, t, :],
                                     start=(t == 0), stop=False)
                    nc.tensor.matmul(bank[6 + r][:, 0:D], ph, c_lo[:, slot, t, :],
                                     start=False, stop=False)
                    last = nc.tensor.matmul(bank[6 + r][:, 0:D], pl, c_hi[:, slot, t, :],
                                            start=False, stop=(t == nt - 1))
                last.then_inc(pv_ps, 1)

            def step(loop, i):
                if i + 1 < GROUPS:
                    transpose_ctx(loop, i + 1, (i + 1) % RING)
                if i < GROUPS:
                    scores(loop, i, GT * P if loop is not None else tiles_of(i) * P)
                if 1 <= i <= GROUPS:
                    transpose_prob(loop, i - 1, GT if loop is not None else tiles_of(i - 1))
                if i >= 2:
                    weigh(loop, i - 2, (i - 2) % RING, GT if loop is not None else tiles_of(i - 2))

            transpose_ctx(None, 0, 0)
            spectrum(1)
            for i in range(FIRST):
                step(None, i)
            with pe.Fori(0, LOOPS) as n:
                for u in range(RING):
                    step(n, FIRST + u)
            for i in range(FIRST + RING * LOOPS, GROUPS + 2):
                step(None, i)

            transpose_xh(pe, 1)
            pe.wait_ge(xhT_rdy, 2)
            pe.wait_ge(ld_pw, 32)

            def project(lo, hi, b):
                for k in range(DK):
                    last = nc.tensor.matmul(bank[b][:, 0:hi - lo], xhT[:, k, :], pw[:, k, lo:hi],
                                            start=(k == 0), stop=(k == DK - 1))
                last.then_inc(proj_ps, 1)

            project(0, D, 2)
            for o in range(ORDER):
                pe.wait_ge(v_rdy, o + 1)
                nc.tensor.matmul(bank[4][:, 0:D], dft_c, vbuf[:, o, :], start=True, stop=True)
                nc.tensor.matmul(bank[4][:, D:2 * D], dft_s, vbuf[:, o, :], start=True, stop=True
                                 ).then_inc(freq_ps, 1)
                if o == 0:
                    project(D, 3 * D, 3)
                for half, inv in ((0, inv_s), (1, inv_c)):
                    pe.wait_ge(prod_rdy, 2 * o + half + 1)
                    for part in range(2):
                        last = nc.tensor.matmul(bank[5][:, 0:D], inv, prod[:, half, part * D:(part + 1) * D],
                                                start=(half == 0 and part == 0),
                                                stop=(half == 1 and part == 1))
                last.then_inc(conv_ps, 1)
            pe.wait_ge(se_rdy, 1)
            for n in range(4):
                k, half = n // 2, n % 2
                for j in range(4):
                    last = nc.tensor.transpose(bank[SE_BANK[n]][:, j * P:(j + 1) * P],
                                               se[:, 4 * half + j, k * P:(k + 1) * P], ident)
                last.then_inc(seT_ps, 1)

            pe.wait_ge(z_rdy, 1)
            for k in range(DK):
                last = nc.tensor.transpose(bank[1][:, k * P:(k + 1) * P], xh[:, k * P:(k + 1) * P], ident)
            last.then_inc(zT_ps, 1)
            pe.wait_ge(xnT_rdy, DK)
            pe.wait_ge(seT_rdy, 4)
            for half in range(2):
                for k in range(DK):
                    last = nc.tensor.matmul(bank[3 + half][:, :], xnT[:, k, :],
                                            seT[:, k, half * 512:(half + 1) * 512],
                                            start=(k == 0), stop=(k == DK - 1))
                last.then_inc(L_ps, 1)
            for half in range(2):
                pe.wait_ge((L0_rdy, L1_rdy)[half], 1)
                for j in range(4):
                    c = 4 * half + j
                    last = nc.tensor.transpose(bank[6 + half][:, j * P:(j + 1) * P],
                                               comb[:, c * P:(c + 1) * P], ident)
                last.then_inc(LT_ps, 1)

            def dispatch_half(half):
                pe.wait_ge(dT_rdy, half + 1)
                b = (0, 2)[half]
                for j in range(4):
                    last = nc.tensor.transpose(bank[b][:, j * P:(j + 1) * P], dT[:, 4 * half + j, :], ident)
                last.then_inc(disp_ps, 1)
                pe.wait_ge(disp_rdy, half + 1)
                pe.wait_ge(xn_rdy, 1)
                for k in range(DK):
                    if half == 1:
                        pe.wait_ge(slots_rdy[k], 1)
                    nc.tensor.matmul(bank[(1, 5)[k]][:, :], xn[:, k * P:(k + 1) * P],
                                     disp[:, half * 512:(half + 1) * 512],
                                     start=True, stop=True).then_inc(slots_ps, 1)

            def combine_transpose(half):
                pe.wait_ge(cexp_rdy, half + 1)
                if half == 0:
                    pe.wait_ge(slots_rdy[1], 2)
                else:
                    pe.wait_ge(combT_rdy, 1)
                for j in range(4):
                    c = 4 * half + j
                    last = nc.tensor.transpose(bank[5][:, j * P:(j + 1) * P], comb[:, c * P:(c + 1) * P], ident)
                last.then_inc(combT_ps, 1)

            dispatch_half(0)

            def hidden_of(p, which, b, done):
                s = p % WSLOTS
                pe.wait_ge(ld_wgu[s], 32 * (p // WSLOTS + 1))
                for k in range(DK):
                    for a in range(2):
                        last = nc.tensor.matmul(bank[b][a * SL:(a + 1) * SL, :],
                                                slotsT[:, k, p * P + a * SL:p * P + (a + 1) * SL],
                                                w_gu[s][:, which, a, k, :], start=(k == 0), stop=(k == DK - 1))
                last.then_inc(done, 1)

            def down_of(p):
                s = p % WSLOTS
                pe.wait_ge(hidT_rdy, p + 1)
                pe.wait_ge(ld_wd[s], 16 * (p // WSLOTS + 1))
                if p >= 1:
                    pe.wait_ge(eout_rdy, p)
                for c in range(FC):
                    for a in range(2):
                        last = nc.tensor.matmul(bank[4][a * SL:(a + 1) * SL, 0:D],
                                                hidT[:, c, a * SL:(a + 1) * SL], w_d[s][:, a, c, :],
                                                start=(c == 0), stop=(c == FC - 1))
                last.then_inc(down_ps, 1)

            def hidden_transpose(p):
                pe.wait_ge(hid_rdy, p + 1)
                if p >= 1:
                    pe.wait_ge(hidT_rdy, p)
                for c in range(FC):
                    last = nc.tensor.transpose(bank[3][:, c * P:(c + 1) * P], hid[:, c * P:(c + 1) * P], ident)
                last.then_inc(hidT_ps, 1)

            def mix_of(p):
                pe.wait_ge(eout_rdy, p + 1)
                if p == 0:
                    pe.wait_ge(combT_rdy, 2)
                last = nc.tensor.matmul(bank[1][:, 0:D], combT[:, p, :], eout[:, :],
                                        start=(p == 0), stop=(p == PAIRS - 1))
                last.then_inc(mix_ps, 1)

            for p in range(PAIRS + 1):
                if p < PAIRS:
                    if p % 4 == 0:
                        for k in range(DK):
                            pe.wait_ge(slots_rdy[k], p // 4 + 1)
                    if p >= 2:
                        pe.wait_ge(gate_rdy, p - 1)
                    hidden_of(p, 0, (6, 7)[p % 2], gate_ps)
                if p == 0:
                    dispatch_half(1)
                if p >= 1:
                    hidden_transpose(p - 1)
                if p < PAIRS:
                    if p >= 2:
                        pe.wait_ge(up_rdy, p - 1)
                    hidden_of(p, 1, (0, 2)[p % 2], up_ps)
                if p == 1:
                    combine_transpose(0)
                if p >= 2:
                    mix_of(p - 2)
                if p >= 1:
                    down_of(p - 1)
                if p == 1:
                    combine_transpose(1)
            mix_of(PAIRS - 1)

        @block.scalar
        def _(act):
            act.dma_start(scale_b[:, :], scale.rearrange("(a n) -> a n", a=1).broadcast_to([P, 1])
                          ).then_inc(ld_scale, 16)
            act.dma_start(filt[:, :, :], filter_time[:, 0, 0:P, :].rearrange("o t d -> t o d")
                          ).then_inc(ld_filt, 16)
            act.dma_start(se, slot_embeds.rearrange("(j a) s d -> (a s) j d", a=2)).then_inc(ld_se, 16)
            act.wait_ge(WT_ps, 1)
            nc.scalar.activation(WT[:, :, :].rearrange("p k e -> p (k e)"), bank[0][:, :], ACT.Copy
                                 ).then_inc(WT_rdy, 1)
            act.wait_ge(q_ps, 1)
            nc.scalar.activation(q_hi[:, :, :].rearrange("p k q -> p (k q)"), bank[3][:, 0:D], ACT.Copy
                                 ).then_inc(qhi_rdy, 1)
            act.dma_start(pw[:, :, :], proj_w.rearrange("(k p) e -> p k e", p=P)).then_inc(ld_pw, 16)
            act.dma_start(pb[:, :], proj_b.rearrange("(a n) -> a n", a=1).broadcast_to([P, 3 * D])
                          ).then_inc(ld_pw, 16)
            for i, v in enumerate((norm_g, norm_b)):
                act.dma_start(g_row[:, i, :], v.rearrange("(a n) -> a n", a=1).broadcast_to([P, D])
                              ).then_inc(ld_row, 16)

            def spectrum(o):
                act.wait_ge(spec_ps, o + 1)
                nc.scalar.activation(spec[:, o, 0:2, :].rearrange("p a d -> p (a d)"), bank[4 + o][:, :], ACT.Copy
                                     ).then_inc(spec_rdy, 1)
                nc.scalar.activation(spec[:, o, 2, :], bank[4 + o][:, 0:D], ACT.Copy, scale=-1.0
                                     ).then_inc(spec_rdy, 1)

            def ctx_hi(loop, g, n):
                for h in range(DK):
                    act.wait_ge(cT_ps, twice(loop, 2 * g + h + 1))
                    if g >= 2:
                        act.wait_ge(score_ps, times(loop, g - 1))
                    nc.scalar.activation(cT_hi[:, g % 2, h, 0:n], bank[h][:, 0:n], ACT.Copy
                                         ).then_inc(cThi_rdy, 1)

            def rows_hi(loop, g, slot, nt):
                act.wait_ge(ld_raw[slot], raw_count(loop, g))
                if loop is not None or g >= RING:
                    act.wait_ge(pv_ps, times(loop, g - RING + 1))
                nc.scalar.activation(c_hi[:, slot, nt // 2:nt, :], raw[:, slot, nt // 2:nt, :], ACT.Copy
                                     ).then_inc(chi2_rdy, 1)

            def prob_hi(loop, g, n):
                act.wait_ge(pT_ps, times(loop, g + 1))
                if g >= 2:
                    act.wait_ge(pv_ps, times(loop, g - 1))
                nc.scalar.activation(pT_hi[:, g % 2, 0:n], bank[4 + g % 2][:, 0:n], ACT.Copy
                                     ).then_inc(pThi_rdy, 1)

            def exps(loop, g, n):
                act.wait_ge(ebias_rdy, times(loop, g + 1))
                if g >= 2:
                    act.wait_ge(pT_ps, times(loop, g - 1))
                nc.scalar.activation(prob[:, g % 2, 0:n], bank[2 + g % 2][:, 0:n], ACT.Exp,
                                     bias=ebias[:, g % RING:g % RING + 1],
                                     accum_out=rsum[:, g % RING:g % RING + 1]).then_inc(prob_rdy, 1)
                nc.scalar.activation(alpha[:, g % RING:g % RING + 1],
                                     negm[:, (g - 1) % RING:(g - 1) % RING + 1], ACT.Exp, scale=-1.0,
                                     bias=negm[:, g % RING:g % RING + 1]).then_inc(alpha_rdy, 1)

            def step(loop, i):
                full = loop is not None
                if i + 1 < GROUPS:
                    ctx_hi(loop, i + 1, (GT if full else tiles_of(i + 1)) * P)
                    rows_hi(loop, i + 1, (i + 1) % RING, GT if full else tiles_of(i + 1))
                if 1 <= i <= GROUPS:
                    prob_hi(loop, i - 1, (GT if full else tiles_of(i - 1)) * P)
                if i < GROUPS:
                    exps(loop, i, (GT if full else tiles_of(i)) * P)

            ctx_hi(None, 0, GT * P)
            rows_hi(None, 0, 0, GT)
            spectrum(0)
            spectrum(1)
            for i in range(FIRST):
                step(None, i)
                if i < 2:
                    load_hidden(act, i)
                    load_down(act, i)
            with act.Fori(0, LOOPS) as n:
                for u in range(RING):
                    step(n, FIRST + u)
            for i in range(FIRST + RING * LOOPS, GROUPS + 1):
                step(None, i)

            for n in range(4):
                act.wait_ge(seT_ps, n + 1)
                k, half = n // 2, n % 2
                nc.scalar.activation(seT[:, k, half * 512:(half + 1) * 512], bank[SE_BANK[n]][:, :],
                                     ACT.Identity, scale=col[:, 1, k:k + 1], bias=col[:, 2, k:k + 1]
                                     ).then_inc(seT_rdy, 1)
            act.wait_ge(zT_ps, 1)
            for k in range(DK):
                nc.scalar.activation(xnT[:, k, :], bank[1][:, k * P:(k + 1) * P], ACT.Identity,
                                     scale=col[:, 3, k:k + 1], bias=col[:, 4, k:k + 1]
                                     ).then_inc(xnT_rdy, 1)
            act.wait_ge(L_ps, 2)
            nc.scalar.activation(comb[:, 512:1024], bank[4][:, :], ACT.Copy).then_inc(L1_rdy, 1)
            for half in range(2):
                act.wait_ge(cmax_rdy, half + 1)
                for j in range(4):
                    c = 4 * half + j
                    last = nc.scalar.activation(dT[:, c, :], bank[6 + half][:, j * P:(j + 1) * P], ACT.Exp,
                                                bias=cmax[:, c:c + 1], accum_out=csum[:, c:c + 1])
                last.then_inc(dexp_rdy, 1)
            act.wait_ge(slots_ps, 2)
            nc.scalar.activation(slotsT[:, 1, 0:512], bank[5][:, :], ACT.Copy).then_inc(slots_rdy[1], 1)
            act.wait_ge(rmax_rdy, 1)
            act.wait_ge(LT_ps, 2)
            for half in range(2):
                nc.scalar.activation(comb[:, half * 512:(half + 1) * 512], comb[:, half * 512:(half + 1) * 512],
                                     ACT.Exp, bias=rmax[:, 0:1], accum_out=rs[:, half:half + 1]
                                     ).then_inc(cexp_rdy, 1)
            act.wait_ge(slots_ps, 4)
            nc.scalar.activation(slotsT[:, 1, 512:1024], bank[5][:, :], ACT.Copy).then_inc(slots_rdy[1], 1)

            def combine_copy(half):
                act.wait_ge(combT_ps, half + 1)
                act.wait_ge(disp_ps, 2)
                nc.scalar.activation(combT[:, 4 * half:4 * half + 4, :].rearrange("p j n -> p (j n)"),
                                     bank[5][:, :], ACT.Copy).then_inc(combT_rdy, 1)

            for p in range(PAIRS):
                act.wait_ge(gate_rdy, p + 1)
                nc.scalar.activation(gate[:, p % 2, :], gate[:, p % 2, :], ACT.Gelu).then_inc(gelu_rdy, 1)
                act.wait_ge(hidT_ps, p + 1)
                if p >= 1:
                    act.wait_ge(down_ps, p)
                nc.scalar.activation(hidT[:, :, :].rearrange("p c s -> p (c s)"), bank[3][:, :], ACT.Copy
                                     ).then_inc(hidT_rdy, 1)
                if p == 0:
                    combine_copy(0)
                    combine_copy(1)

        @block.gpsimd
        def _(pool):
            nc.gpsimd.memset(neg_half[:, :], -0.5).then_inc(half_set, 1)
            nc.gpsimd.memset(zero[:, :], 0.0).then_inc(half_set, 1)
            pool.wait_ge(half_set, 2)

            def power(n, dst, src, width):
                pool.wait_ge(var_rdy, n + 1)
                nc.gpsimd.tensor_tensor(dst, src, neg_half[:, 0:width], ALU.pow).then_inc(rstd_rdy, 1)

            power(0, rstd[:, 0:1], mv[:, 1:2], 1)

            def split_ctx(loop, g, slot, nt):
                pool.wait_ge(ld_raw[slot], raw_count(loop, g))
                if loop is not None or g >= RING:
                    pool.wait_ge(pv_ps, times(loop, g - RING + 1))
                nc.gpsimd.tensor_tensor(c_hi[:, slot, 0:nt // 2, :].rearrange("p t d -> p (t d)"),
                                        raw[:, slot, 0:nt // 2, :].rearrange("p t d -> p (t d)"),
                                        zero[:, 0:1].broadcast_to([P, nt // 2 * D]), ALU.add).then_inc(chi_rdy, 1)
                pool.wait_ge(chi_rdy, times(loop, g + 1))
                pool.wait_ge(chi2_rdy, times(loop, g + 1))
                nc.gpsimd.tensor_tensor(c_lo[:, slot, 0:nt, :], raw[:, slot, 0:nt, :],
                                        c_hi[:, slot, 0:nt, :].bitcast(fp32), ALU.subtract
                                        ).then_inc(clo_rdy, 1)

            for g in range(RING):
                split_ctx(None, g, g, GT)
                if g == 2:
                    power(1, se_rstd[:, :], se_mv[:, :, 1], PAIRS)
            with pool.Fori(0, LOOPS) as n:
                for u in range(RING):
                    split_ctx(n, RING + u, u, GT)
            split_ctx(None, LAST, LAST % RING, LAST_T)
            power(2, rstd[:, 0:1], mv[:, 1:2], 1)
            for p in range(BSLOTS):
                load_bias(pool, p)
            for n in range(3, 5):
                power(n, rstd[:, 0:1], mv[:, 1:2], 1)
            for p in range(BSLOTS, PAIRS):
                pool.wait_ge(eout_rdy, p - BSLOTS + 1)
                load_bias(pool, p)

        @block.vector
        def _(dve):
            count = [0]

            def link(ins):
                count[0] += 1
                ins.then_inc(dve_n, 1)
                dve.wait_ge(dve_n, count[0])

            def norm(n, src, dst, done):
                link(nc.vector.bn_stats(stat6[:, :], src))
                link(nc.vector.bn_aggr(mv[:, :], stat6[:, :]))
                nc.vector.tensor_scalar(mv[:, 1:2], mv[:, 1:2], EPS, None, ALU.add).then_inc(var_rdy, 1)
                dve.wait_ge(rstd_rdy, n + 1)
                last = nc.vector.tensor_scalar(dst, src, mv[:, 0:1], rstd[:, 0:1], ALU.subtract, ALU.mult)
                if done is None:
                    link(last)
                else:
                    last.then_inc(done, 1)

            dve.wait_ge(ld_x, 16)
            norm(0, x_sb[:, :], xh[:, :], xh_rdy)
            dve.wait_ge(xhT_ps, 1)
            nc.vector.tensor_copy(xhT[:, :, :].rearrange("p k t -> p (k t)"), bank[1][:, 0:D]).then_inc(xhT_rdy, 1)
            dve.wait_ge(ld_col, 16)
            dve.wait_ge(exT_ps, 1)
            for e in range(DK):
                last = nc.vector.tensor_scalar(exT[:, e, :], bank[2][:, e * P:(e + 1) * P], col[:, 0, e:e + 1],
                                               None, ALU.add)
            last.then_inc(exT_rdy, 1)
            dve.wait_ge(qhi_rdy, 1)
            nc.vector.tensor_tensor(q_lo[:, :, :].rearrange("p k q -> p (k q)"), bank[3][:, 0:D],
                                    q_hi[:, :, :].rearrange("p k q -> p (k q)").bitcast(fp32), ALU.subtract
                                    ).then_inc(q_rdy, 1)
            nc.vector.tensor_copy(s0[:, :], bank[3][:, 2 * P:2 * P + 1]).then_inc(s0_rdy, 1)
            nc.vector.memset(negm[:, RING - 1:RING], BIG)
            nc.vector.memset(lsum[:, :], 0.0)
            nc.vector.memset(O[:, :], 0.0).then_inc(O_upd, 1)
            dve.wait_ge(ld_scale, 16)
            for i in (1, 2):
                last = nc.vector.tensor_scalar(col[:, i, :], col[:, i, :], scale_b[:, 0:1], None, ALU.mult)
            last.then_inc(gs_rdy, 1)

            def slot_stats(tiles):
                dve.wait_ge(ld_se, 16)
                for j in tiles:
                    last = nc.vector.bn_stats(se_stat[:, j, :], se[:, j, :])
                link(last)

            def slot_variance():
                for j in range(PAIRS):
                    last = nc.vector.bn_aggr(se_mv[:, j, :], se_stat[:, j, :])
                link(last)
                nc.vector.tensor_scalar(se_mv[:, :, 1], se_mv[:, :, 1], EPS, None, ALU.add).then_inc(var_rdy, 1)

            def slot_norm(tiles):
                dve.wait_ge(rstd_rdy, 2)
                for j in tiles:
                    last = nc.vector.tensor_scalar(se[:, j, :], se[:, j, :], se_mv[:, j, 0:1],
                                                   se_rstd[:, j:j + 1], ALU.subtract, ALU.mult)
                if PAIRS - 1 in tiles:
                    last.then_inc(se_rdy, 1)

            def ctx_lo(loop, g, n):
                for h in range(DK):
                    dve.wait_ge(cThi_rdy, twice(loop, 2 * g + h + 1))
                    nc.vector.tensor_tensor(cT_lo[:, g % 2, h, 0:n], bank[h][:, 0:n],
                                            cT_hi[:, g % 2, h, 0:n].bitcast(fp32), ALU.subtract
                                            ).then_inc(cTlo_rdy, 1)

            def running_max(loop, g, n):
                r = g % RING
                dve.wait_ge(score_ps, times(loop, g + 1))
                nc.vector.tensor_reduce(gmax[:, :], bank[2 + g % 2][:, 0:n], AX.X, ALU.max, negate=True
                                        ).then_inc(gmax_rdy, 1)
                dve.wait_ge(gmax_rdy, times(loop, g + 1))
                nc.vector.scalar_tensor_tensor(out=negm[:, r:r + 1], in0=gmax[:, :], scalar=s0[:, 0:1],
                                               in1=negm[:, (g - 1) % RING:(g - 1) % RING + 1],
                                               op0=ALU.subtract, op1=ALU.min).then_inc(negm_rdy, 1)
                dve.wait_ge(negm_rdy, times(loop, g + 1))
                nc.vector.tensor_tensor(ebias[:, r:r + 1], negm[:, r:r + 1], s0[:, :], ALU.add
                                        ).then_inc(ebias_rdy, 1)

            def prob_lo(loop, g, n):
                dve.wait_ge(pThi_rdy, times(loop, g + 1))
                nc.vector.tensor_tensor(pT_lo[:, g % 2, 0:n], bank[4 + g % 2][:, 0:n],
                                        pT_hi[:, g % 2, 0:n].bitcast(fp32), ALU.subtract).then_inc(pTlo_rdy, 1)

            def update(loop, g):
                r = g % RING
                dve.wait_ge(alpha_rdy, times(loop, g + 1))
                if g >= 1:
                    dve.wait_ge(l_upd, times(loop, g))
                nc.vector.scalar_tensor_tensor(out=lsum[:, :], in0=lsum[:, :], scalar=alpha[:, r:r + 1],
                                               in1=rsum[:, r:r + 1], op0=ALU.mult, op1=ALU.add).then_inc(l_upd, 1)
                dve.wait_ge(pv_ps, times(loop, g + 1))
                dve.wait_ge(O_upd, times(loop, g + 1))
                nc.vector.scalar_tensor_tensor(out=O[:, :], in0=O[:, :], scalar=alpha[:, r:r + 1],
                                               in1=bank[6 + g % 2][:, 0:D], op0=ALU.mult, op1=ALU.add
                                               ).then_inc(O_upd, 1)

            def step(loop, i):
                full = loop is not None
                if i + 1 < GROUPS:
                    ctx_lo(loop, i + 1, (GT if full else tiles_of(i + 1)) * P)
                if i < GROUPS:
                    running_max(loop, i, (GT if full else tiles_of(i)) * P)
                if 1 <= i <= GROUPS:
                    prob_lo(loop, i - 1, (GT if full else tiles_of(i - 1)) * P)
                if i >= 2:
                    update(loop, i - 2)

            dve.wait_ge(s0_rdy, 1)
            ctx_lo(None, 0, GT * P)
            for i in range(FIRST):
                step(None, i)
                if i < 2:
                    slot_stats(range(4 * i, 4 * i + 4))
                else:
                    slot_variance()
            with dve.Fori(0, LOOPS) as n:
                for u in range(RING):
                    step(n, FIRST + u)
            for i in range(FIRST + RING * LOOPS, GROUPS + 2):
                step(None, i)
                if i < GROUPS + 1:
                    j = i - FIRST - RING * LOOPS
                    slot_norm(range(3 * j, min(3 * j + 3, PAIRS)))

            dve.wait_ge(l_upd, GROUPS)
            dve.wait_ge(O_upd, GROUPS + 1)
            link(nc.vector.reciprocal(linv[:, :], lsum[:, :]))
            link(nc.vector.scalar_tensor_tensor(out=x1[:, :], in0=O[:, :], scalar=linv[:, 0:1], in1=x_sb[:, :],
                                                op0=ALU.mult, op1=ALU.add))
            norm(2, x1[:, :], xh[:, :], xh_rdy)
            dve.wait_ge(xhT_ps, 2)
            nc.vector.tensor_copy(xhT[:, :, :].rearrange("p k t -> p (k t)"), bank[1][:, 0:D]).then_inc(xhT_rdy, 1)
            dve.wait_ge(ld_pw, 32)
            dve.wait_ge(proj_ps, 1)
            nc.vector.tensor_tensor(vbuf[:, 0, :], bank[2][:, 0:D], pb[:, 0:D], ALU.add).then_inc(v_rdy, 1)
            for o in range(ORDER):
                dve.wait_ge(freq_ps, o + 1)
                for half in range(2):
                    nc.vector.tensor_tensor(prod[:, half, :], bank[4][:, :],
                                            spec[:, o, half:half + 2, :].rearrange("p a d -> p (a d)"), ALU.mult
                                            ).then_inc(prod_rdy, 1)
                if o == 0:
                    dve.wait_ge(proj_ps, 2)
                    link(nc.vector.tensor_tensor(p_sb[:, D:3 * D], bank[3][:, :], pb[:, D:3 * D], ALU.add))
                dve.wait_ge(conv_ps, o + 1)
                if o + 1 < ORDER:
                    nc.vector.tensor_tensor(vbuf[:, o + 1, :], bank[5][:, 0:D], p_sb[:, (o + 1) * D:(o + 2) * D],
                                            ALU.mult).then_inc(v_rdy, 1)
                else:
                    link(nc.vector.tensor_tensor(xn[:, :], bank[5][:, 0:D], p_sb[:, (o + 1) * D:(o + 2) * D],
                                                 ALU.mult))
            link(nc.vector.tensor_tensor(x2[:, :], x1[:, :], xn[:, :], ALU.add))
            norm(3, x2[:, :], xn[:, :], None)
            norm(4, xn[:, :], xh[:, :], z_rdy)
            dve.wait_ge(ld_row, 32)
            dve.wait_ge(z_rdy, 1)
            link(nc.vector.tensor_tensor(xn[:, :], xh[:, :], g_row[:, 0, :], ALU.mult))
            nc.vector.tensor_tensor(xn[:, :], xn[:, :], g_row[:, 1, :], ALU.add).then_inc(xn_rdy, 1)
            dve.wait_ge(L_ps, 1)
            nc.vector.tensor_copy(comb[:, 0:512], bank[3][:, :]).then_inc(L0_rdy, 1)
            for half in range(2):
                dve.wait_ge(LT_ps, half + 1)
                nc.vector.tensor_reduce(cmax[:, 4 * half:4 * half + 4],
                                        bank[6 + half][:, :].rearrange("p (j n) -> p j n", n=P), AX.X, ALU.max,
                                        negate=True).then_inc(cmax_rdy, 1)

            def dispatch_norm(half):
                hs = slice(4 * half, 4 * half + 4)
                dve.wait_ge(dexp_rdy, half + 1)
                link(nc.vector.reciprocal(cinv[:, hs], csum[:, hs]))
                nc.vector.tensor_tensor(dT[:, hs, :], dT[:, hs, :],
                                        cinv[:, hs].unsqueeze(2).broadcast_to([P, 4, P]), ALU.mult
                                        ).then_inc(dT_rdy, 1)

            def dispatch_copy(half):
                dve.wait_ge(disp_ps, half + 1)
                nc.vector.tensor_copy(disp[:, half * 512:(half + 1) * 512], bank[(0, 2)[half]][:, :]
                                      ).then_inc(disp_rdy, 1)

            def slots_copy(half):
                dve.wait_ge(slots_ps, 2 * half + 1)
                nc.vector.tensor_copy(slotsT[:, 0, half * 512:(half + 1) * 512], bank[1][:, :]
                                      ).then_inc(slots_rdy[0], 1)

            dispatch_norm(0)
            dispatch_copy(0)
            dispatch_norm(1)
            slots_copy(0)
            dve.wait_ge(L1_rdy, 1)
            dve.wait_ge(L0_rdy, 1)
            nc.vector.tensor_reduce(rmax[:, :], comb[:, :], AX.X, ALU.max, negate=True).then_inc(rmax_rdy, 1)
            dispatch_copy(1)
            for p in range(PAIRS + 1):
                if p < PAIRS:
                    dve.wait_ge(ld_bias[p % BSLOTS], 32 * (p // BSLOTS + 1))
                    dve.wait_ge(gate_ps, p + 1)
                    if p >= 2:
                        dve.wait_ge(hid_rdy, p - 1)
                    nc.vector.tensor_tensor(gate[:, p % 2, :], bank[(6, 7)[p % 2]][:, :],
                                            bias[:, p % BSLOTS, 0:F], ALU.add
                                            ).then_inc(gate_rdy, 1)
                    if p == 0:
                        slots_copy(1)
                    dve.wait_ge(up_ps, p + 1)
                    if p >= 1:
                        dve.wait_ge(hid_rdy, p)
                    nc.vector.tensor_tensor(up[:, :], bank[(0, 2)[p % 2]][:, :],
                                            bias[:, p % BSLOTS, F:2 * F], ALU.add
                                            ).then_inc(up_rdy, 1)
                    dve.wait_ge(up_rdy, p + 1)
                    dve.wait_ge(gelu_rdy, p + 1)
                    if p >= 1:
                        dve.wait_ge(hidT_ps, p)
                    nc.vector.tensor_tensor(hid[:, :], gate[:, p % 2, :], up[:, :], ALU.mult).then_inc(hid_rdy, 1)
                if p >= 1:
                    dve.wait_ge(down_ps, p)
                    if p >= 2:
                        dve.wait_ge(mix_ps, p - 1)
                    nc.vector.tensor_tensor(eout[:, :], bank[4][:, 0:D],
                                            bias[:, (p - 1) % BSLOTS, 2 * F:2 * F + D], ALU.add
                                            ).then_inc(eout_rdy, 1)
            dve.wait_ge(mix_ps, PAIRS)
            dve.wait_ge(cexp_rdy, 2)
            link(nc.vector.tensor_tensor(rs[:, 2:3], rs[:, 0:1], rs[:, 1:2], ALU.add))
            link(nc.vector.reciprocal(rs[:, 3:4], rs[:, 2:3]))
            nc.vector.scalar_tensor_tensor(out=x1[:, :], in0=bank[1][:, 0:D], scalar=rs[:, 3:4], in1=x2[:, :],
                                           op0=ALU.mult, op1=ALU.add).then_inc(res_rdy, 1)


def spectrum_tables(np, n):
    t = np.arange(n)[:, None]
    w = 2.0 * np.pi * (np.arange(n)[None, :] + 0.5) / (2 * n)
    c, s = np.cos(t * w), np.sin(t * w)
    return np.stack([np.eye(n), c, s, c.T / n, s.T / n], axis=1).astype(np.float32)


_INS = ['x', 'ctx_1024', 'L0_xattn_W', 'L0_attn_proj_w', 'L0_attn_proj_b', 'L0_attn_filter_time',
        'L0_ffn_norm_g', 'L0_ffn_norm_b', 'L0_ffn_scale', 'L0_ffn_slot_embeds', 'L0_ffn_Wg', 'L0_ffn_Wu', 'L0_ffn_Wd']


def kernel(**inputs):
    import numpy as _np
    import concourse.bacc as _bacc
    from concourse import mybir as _mybir
    from concourse.bass_utils import run_bass_kernel_spmd as _run

    nc = _bacc.Bacc("TRN2", target_bir_lowering=False, num_devices=1)
    arrays, args = {}, []

    def add(name, a):
        arrays[name] = a
        args.append(nc.dram_tensor(name, a.shape, _mybir.dt.from_np(a.dtype), kind="ExternalInput").ap())

    for name in _INS:
        add(f"in_{name}_dram", _np.ascontiguousarray(inputs[name]))
    add("biases_dram", _np.concatenate([_np.asarray(inputs[n]) for n in ('L0_ffn_bg', 'L0_ffn_bu', 'L0_ffn_bd')], 1))
    vectors = [inputs[n] for n in ('L0_xattn_b', 'L0_ffn_slot_g', 'L0_ffn_slot_b', 'L0_ffn_norm_g', 'L0_ffn_norm_b')]
    add("columns_dram", _np.ascontiguousarray(_np.stack(
        [_np.asarray(v).reshape(2, 128).transpose(1, 0) for v in vectors], axis=1)))
    add("tables_dram", spectrum_tables(_np, 128))
    args.append(nc.dram_tensor("out_0_dram", (1, 128, 256), _mybir.dt.from_np(_np.dtype("float32")),
                               kind="ExternalOutput").ap())
    perceiver_kernel(nc, *args)
    return _run(nc, [arrays], core_ids=[0]).results[0]["out_0_dram"]
```

```python
import concourse.bass as bass
from concourse import mybir
from contextlib import ExitStack


def perceiver_kernel(nc, x, ctx_in, xattn_W, proj_w, proj_b, filter_time, norm_g, norm_b,
                     scale, slot_embeds, Wg, Wu, Wd, biases, columns, tables, out):
    fp32 = mybir.dt.float32
    fp32r = mybir.dt.float32r
    ALU = mybir.AluOpType
    ACT = mybir.ActivationFunctionType
    AX = mybir.AxisListType

    P = 128
    D = x.shape[2]
    DK = D // P
    KEYS = ctx_in.shape[1]
    TILES = KEYS // P
    GT = 4
    GROUPS = -(-TILES // GT)
    LAST = GROUPS - 1
    LAST_T = TILES - LAST * GT
    RING = 4
    LOOPS = (GROUPS - 5) // RING
    FIRST = 3
    ORDER = filter_time.shape[0]
    E, SL = slot_embeds.shape[0], slot_embeds.shape[1]
    F = Wg.shape[2]
    FC = F // P
    PAIRS = E * SL // P
    SLOTS = E * SL
    WSLOTS = 6
    EARLY = 2
    BSLOTS = 3
    PIECES = ((0, 1), (1, 4), (4, 8))
    FEED = 2 * EARLY
    EPS = 1e-5
    BIG = 3.0e38

    def tiles_of(g):
        return LAST_T if g == LAST else GT

    st = ExitStack()
    with st:
        def sem(name):
            return st.enter_context(nc.semaphore(name))

        def sb(name, shape, dt=fp32, where=st):
            return where.enter_context(nc.sbuf_tensor(name, shape, dt))

        bank = [st.enter_context(nc.psum_tensor(f"bank{i}", [P, 512], fp32)) for i in range(8)]

        tab = sb("tab", [P, 5, P])
        ident, dft_c, dft_s, inv_c, inv_s = (tab[:, i, :] for i in range(5))
        x_sb = sb("x_sb", [P, D])
        x1 = sb("x1", [P, D])
        x2 = sb("x2", [P, D])
        xh = sb("xh", [P, D])
        xhT = sb("xhT", [P, DK, P])
        xn = sb("xn", [P, D])
        xnT = sb("xnT", [P, DK, P])
        stat6 = sb("stat6", [P, 6])
        mv = sb("mv", [P, 2])
        rstd = sb("rstd", [P, 1])
        neg_half = sb("neg_half", [P, PAIRS])
        zero = sb("zero", [P, 1])
        col = sb("col", [P, 5, DK])
        scale_b = sb("scale_b", [P, 1])
        g_row = sb("g_row", [P, 2, D])
        negm = sb("negm", [P, RING])
        ebias = sb("ebias", [P, RING])
        gmax = sb("gmax", [P, 1])
        rsum = sb("rsum", [P, RING])
        alpha = sb("alpha", [P, RING])
        s0 = sb("s0", [P, 1])
        lsum = sb("lsum", [P, 1])
        linv = sb("linv", [P, 1])
        O = sb("O", [P, D])
        slots_or_se = sb("slots_or_se", [P, DK * SLOTS])
        se = slots_or_se[:, :].rearrange("p (j d) -> p j d", d=D)
        slotsT = slots_or_se[:, :].rearrange("p (k s) -> p k s", k=DK)
        se_stat = sb("se_stat", [P, PAIRS, 6])
        se_mv = sb("se_mv", [P, PAIRS, 2])
        se_rstd = sb("se_rstd", [P, PAIRS])
        mid = ExitStack()
        pw = sb("pw", [P, DK, 3 * D], fp32, mid)
        pb = sb("pb", [P, 3 * D], fp32, mid)
        filt = sb("filt", [P, ORDER, D], fp32, mid)
        spec = sb("spec", [P, ORDER, 3, D], fp32, mid)
        seT = sb("seT", [P, DK, SLOTS], fp32, mid)
        mid.close()
        last_gu = sb("last_gu", [P, 2, 2, DK, F])
        last_d = sb("last_d", [P, 2, FC, D])
        eout = sb("eout", [P, 2, D])

        early_gu = sb("early_gu", [P, 2, 2 * EARLY, DK, F])
        early_d = sb("early_d", [P, 2 * EARLY, FC, D])
        bias = sb("bias", [P, BSLOTS, 2 * F + D])

        att = ExitStack()
        raw = sb("raw", [P, RING, GT, D], fp32, att)
        cT_hi = sb("cT_hi", [P, 2, DK, GT * P], fp32r, att)
        cT_lo = sb("cT_lo", [P, 2, DK, GT * P], fp32r, att)
        q_hi = sb("q_hi", [P, DK, P], fp32r, att)
        q_lo = sb("q_lo", [P, DK, P], fp32r, att)
        pre = ExitStack()
        W_sb = sb("W_sb", [P, DK, D], fp32, pre)
        WT = sb("WT", [P, DK, D], fp32, pre)
        exT = sb("exT", [P, DK, P], fp32, pre)
        pre.close()
        prob = sb("prob", [P, 2, GT * P], fp32, att)
        pT_hi = sb("pT_hi", [P, 2, GT * P], fp32r, att)
        pT_lo = sb("pT_lo", [P, 2, GT * P], fp32r, att)
        c_hi = sb("c_hi", [P, RING, GT, D], fp32r, att)
        c_lo = sb("c_lo", [P, RING, GT, D], fp32r, att)
        att.close()
        ffn = ExitStack()
        late_gu = [sb(f"late_gu{i}", [P, 2, 2, DK, F], fp32, ffn) for i in range(EARLY, WSLOTS - 1)] + [last_gu]
        late_d = [sb(f"late_d{i}", [P, 2, FC, D], fp32, ffn) for i in range(EARLY, WSLOTS - 1)] + [last_d]
        dT = sb("dT", [P, PAIRS, P], fp32, ffn)
        combT = dT
        disp = sb("disp", [P, SLOTS], fp32, ffn)
        comb = sb("comb", [P, SLOTS], fp32, ffn)
        cmax = sb("cmax", [P, PAIRS], fp32, ffn)
        csum = sb("csum", [P, PAIRS], fp32, ffn)
        cinv = sb("cinv", [P, PAIRS], fp32, ffn)
        rmax = sb("rmax", [P, 1], fp32, ffn)
        rs = sb("rs", [P, 4], fp32, ffn)
        conv = ExitStack()
        p_sb = sb("p_sb", [P, 3 * D], fp32, conv)
        vbuf = sb("vbuf", [P, 2, D], fp32, conv)
        prod = sb("prod", [P, 4, D], fp32, conv)
        conv.close()
        gate = sb("gate", [P, 2, F], fp32, ffn)
        up = sb("up", [P, F], fp32, ffn)
        hid = sb("hid", [P, F], fp32, ffn)
        hidT = sb("hidT", [P, FC, P], fp32, ffn)
        ffn.close()

        ld_ident = sem("ld_ident")
        ld_x, ld_W, ld_tab, ld_scale = sem("ld_x"), sem("ld_W"), sem("ld_tab"), sem("ld_scale")
        ld_se, ld_col, ld_row, ld_filt = sem("ld_se"), sem("ld_col"), sem("ld_row"), sem("ld_filt")
        ld_pw = sem("ld_pw")
        ld_raw = [sem(f"ld_raw{i}") for i in range(RING)]
        ld_early = sem("ld_early")
        ld_wgu = [sem(f"ld_wgu{i}") for i in range(WSLOTS)]
        ld_wd = [sem(f"ld_wd{i}") for i in range(WSLOTS)]
        ld_bias = [sem(f"ld_bias{i}") for i in range(BSLOTS)]
        st_out = sem("st_out")
        dve_n = sem("dve_n")
        const_set = sem("const_set")
        var_rdy, rstd_rdy = sem("var_rdy"), sem("rstd_rdy")
        idle_set = sem("idle_set")
        xh_rdy, xhT_ps, xhT_rdy = sem("xh_rdy"), sem("xhT_ps"), sem("xhT_rdy")
        WT_ps, WT_rdy = sem("WT_ps"), sem("WT_rdy")
        exT_ps, exT_rdy = sem("exT_ps"), sem("exT_rdy")
        q_ps, qhi_rdy, q_rdy, s0_rdy = sem("q_ps"), sem("qhi_rdy"), sem("q_rdy"), sem("s0_rdy")
        stat_rdy = sem("stat_rdy")
        se_rdy, seT_ps, seT_rdy = sem("se_rdy"), sem("seT_ps"), sem("seT_rdy")
        gs_rdy = sem("gs_rdy")
        spec_ps, spec_rdy = sem("spec_ps"), sem("spec_rdy")
        cT_ps, cThi_rdy, cTlo_rdy = sem("cT_ps"), sem("cThi_rdy"), sem("cTlo_rdy")
        score_ps, gmax_rdy, negm_rdy, ebias_rdy = (sem("score_ps"), sem("gmax_rdy"), sem("negm_rdy"),
                                                   sem("ebias_rdy"))
        prob_rdy, alpha_rdy = sem("prob_rdy"), sem("alpha_rdy")
        pT_ps, pThi_rdy, pTlo_rdy = sem("pT_ps"), sem("pThi_rdy"), sem("pTlo_rdy")
        chi_rdy, chi2_rdy, clo_rdy = sem("chi_rdy"), sem("chi2_rdy"), sem("clo_rdy")
        pv_ps, O_upd, l_upd = sem("pv_ps"), sem("O_upd"), sem("l_upd")
        proj_ps, v_rdy, freq_ps = sem("proj_ps"), sem("v_rdy"), sem("freq_ps")
        prod_rdy, conv_ps = sem("prod_rdy"), sem("conv_ps")
        z_rdy, zT_ps, xn_rdy, xnT_rdy = sem("z_rdy"), sem("zT_ps"), sem("xn_rdy"), sem("xnT_rdy")
        L_ps, L_rdy, LT_ps = sem("L_ps"), sem("L_rdy"), sem("LT_ps")
        cmax_rdy, dexp_rdy, dT_rdy = sem("cmax_rdy"), sem("dexp_rdy"), sem("dT_rdy")
        disp_ps, disp_rdy = sem("disp_ps"), sem("disp_rdy")
        slots_ps, slots_rdy = sem("slots_ps"), sem("slots_rdy")
        rmax_rdy, cexp_rdy = sem("rmax_rdy"), sem("cexp_rdy")
        combT_ps, combT_rdy = sem("combT_ps"), sem("combT_rdy")
        gate_ps, up_ps, gate_rdy, up_rdy = sem("gate_ps"), sem("up_ps"), sem("gate_rdy"), sem("up_rdy")
        gelu_rdy, hid_rdy, hidT_ps, hidT_rdy = (sem("gelu_rdy"), sem("hid_rdy"), sem("hidT_ps"),
                                                sem("hidT_rdy"))
        down_ps, eout_rdy, mix_ps, res_rdy = sem("down_ps"), sem("eout_rdy"), sem("mix_ps"), sem("res_rdy")

        ctx_v = ctx_in[0, :, :].rearrange("(p j) d -> p j d", p=P)

        def times(loop, static):
            return static if loop is None else loop * RING + static

        def twice(loop, static):
            return static if loop is None else loop * (2 * RING) + static

        def raw_count(loop, g):
            n = 16 * (g // RING + 1)
            return n if loop is None else loop * 16 + n

        def load_bias(eng, p):
            s = p % BSLOTS
            for a in range(2):
                eng.dma_start(bias[a * SL:(a + 1) * SL, s, :],
                              biases[2 * p + a:2 * p + a + 1, :].broadcast_to([SL, 2 * F + D])
                              ).then_inc(ld_bias[s], 16)

        def w_gu(slot, which, lo, hi):
            if slot < EARLY:
                return early_gu[:, which, 2 * slot + lo:2 * slot + hi, :, :]
            return late_gu[slot - EARLY][:, which, lo:hi, :, :]

        def w_d(slot, lo, hi):
            if slot < EARLY:
                return early_d[:, 2 * slot + lo:2 * slot + hi, :, :]
            return late_d[slot - EARLY][:, lo:hi, :, :]

        def load_hidden(eng, p):
            for i, w in enumerate((Wg, Wu)):
                eng.dma_start(w_gu(p % WSLOTS, i, 0, 2).rearrange("p e k f -> p (e k) f"),
                              w[2 * p:2 * p + 2, :, :].rearrange("e (k p) f -> p (e k) f", p=P)
                              ).then_inc(ld_wgu[p % WSLOTS], 16)

        def load_down(eng, p):
            eng.dma_start(w_d(p % WSLOTS, 0, 2).rearrange("p e c o -> p (e c) o"),
                          Wd[2 * p:2 * p + 2, :, :].rearrange("e (c p) o -> p (e c) o", p=P)
                          ).then_inc(ld_wd[p % WSLOTS], 16)

        XH_BANK = (4, 1)

        def transpose_xh(pe, n):
            pe.wait_ge(xh_rdy, n + 1)
            for k in range(DK):
                last = nc.tensor.transpose(bank[XH_BANK[n]][:, k * P:(k + 1) * P], xh[:, k * P:(k + 1) * P], ident)
            last.then_inc(xhT_ps, 1)

        block = st.enter_context(nc.Block())

        @block.sync
        def _(sp):
            sp.dma_start(x_sb[:, :], x[0, :, :]).then_inc(ld_x, 16)
            sp.dma_start(W_sb[:, :, :], xattn_W.rearrange("(k p) d -> p k d", p=P)).then_inc(ld_W, 16)

            def load_rows(g):
                sp.dma_start(raw[:, g % RING, 0:tiles_of(g), :], ctx_v[:, g * GT:g * GT + tiles_of(g), :]
                             ).then_inc(ld_raw[g % RING], 16)

            load_rows(0)
            load_rows(1)
            sp.dma_start(filt[:, :, :], filter_time[:, 0, 0:P, :].rearrange("o t d -> t o d")
                         ).then_inc(ld_filt, 16)
            sp.dma_start(tab[:, 1:5, :], tables[:, 1:5, :]).then_inc(ld_tab, 16)
            load_rows(2)
            sp.dma_start(se, slot_embeds.rearrange("(j a) s d -> (a s) j d", a=2)).then_inc(ld_se, 16)
            load_rows(3)
            with sp.Fori(0, FEED) as n:
                for u in range(RING):
                    sp.wait_ge(score_ps, n * RING + (u + 1))
                    sp.wait_ge(clo_rdy, n * RING + (u + 1))
                    sp.dma_start(raw[:, u, :, :], ctx_v[:, bass.ds(n * (RING * GT) + (RING + u) * GT, GT), :]
                                 ).then_inc(ld_raw[u], 16)
                    if u < 2:
                        sp.dma_start(early_gu[:, u, bass.ds(n, 1), :, :].rearrange("p e k f -> p (e k) f"),
                                     (Wg, Wu)[u][bass.ds(n, 1), :, :].rearrange("e (k p) f -> p (e k) f", p=P)
                                     ).then_inc(ld_early, 16)
                    elif u == 2:
                        sp.dma_start(early_d[:, bass.ds(n, 1), :, :].rearrange("p e c o -> p (e c) o"),
                                     Wd[bass.ds(n, 1), :, :].rearrange("e (c p) o -> p (e c) o", p=P)
                                     ).then_inc(ld_early, 16)
            for g in range(RING * (FEED + 1), GROUPS):
                sp.wait_ge(score_ps, g - RING + 1)
                sp.wait_ge(clo_rdy, g - RING + 1)
                load_rows(g)
                if g == RING * (FEED + 1):
                    sp.dma_start(pw[:, :, :], proj_w.rearrange("(k p) e -> p k e", p=P)).then_inc(ld_pw, 16)
                    sp.dma_start(pb[:, :], proj_b.rearrange("(a n) -> a n", a=1).broadcast_to([P, 3 * D])
                                 ).then_inc(ld_pw, 16)
                if g == RING * (FEED + 1) + 1:
                    for i, v in enumerate((norm_g, norm_b)):
                        sp.dma_start(g_row[:, i, :], v.rearrange("(a n) -> a n", a=1).broadcast_to([P, D])
                                     ).then_inc(ld_row, 16)
            for p in range(BSLOTS):
                load_bias(sp, p)
            sp.wait_ge(clo_rdy, GROUPS)
            sp.wait_ge(score_ps, GROUPS)
            load_hidden(sp, EARLY)
            load_hidden(sp, EARLY + 1)
            sp.wait_ge(pv_ps, GROUPS)
            load_down(sp, EARLY)
            load_down(sp, EARLY + 1)
            for p in range(EARLY + 2, WSLOTS):
                if p == WSLOTS - 1:
                    sp.wait_ge(z_rdy, 1)
                load_hidden(sp, p)
                if p == WSLOTS - 1:
                    sp.wait_ge(L_ps, len(PIECES))
                load_down(sp, p)

            def reload_hidden(p):
                sp.wait_ge(up_ps, p - WSLOTS + 1)
                load_hidden(sp, p)

            def reload_down(p):
                sp.wait_ge(down_ps, p - WSLOTS + 1)
                load_down(sp, p)

            def reload_bias(p):
                sp.wait_ge(eout_rdy, p - BSLOTS + 1)
                load_bias(sp, p)

            for p in range(WSLOTS, PAIRS):
                reload_hidden(p)
                reload_down(p)
                reload_bias(p - WSLOTS + BSLOTS)
            for p in range(PAIRS - WSLOTS + BSLOTS, PAIRS):
                reload_bias(p)
            sp.wait_ge(res_rdy, 1)
            sp.dma_start(out[0, :, :], x1[:, :]).then_inc(st_out, 16)
            sp.wait_ge(st_out, 16)

        LT_BANK = (6, 7, 0)
        DISP_BANK = (2, 3, 1)
        SLOTS_AT = (((1, 0), (1, P)), ((4, 0), (5, 0)), ((5, 0), (1, 0)))
        UP_BANK = (2, 0)
        SE_BANK = (6, 3, 2, 6)

        @block.tensor
        def _(pe):
            def keep_busy(n):
                for _ in range(n):
                    nc.tensor.transpose(bank[0][:, 0:P], ident, ident)

            pe.wait_ge(idle_set, 1)
            for _ in range(4):
                nc.tensor.matmul(bank[7][:, 0:D], O[:, 0:P], O[:, :], start=True, stop=True)
            pe.wait_ge(ld_ident, 16)
            pe.wait_ge(ld_W, 16)
            for d in range(DK):
                for e in range(DK):
                    last = nc.tensor.transpose(bank[6 + d][:, e * P:(e + 1) * P],
                                               W_sb[:, e, d * P:(d + 1) * P], ident)
                last.then_inc(WT_ps, 1)
            transpose_xh(pe, 0)

            def spectrum(o):
                pe.wait_ge(ld_filt, 16)
                pe.wait_ge(ld_tab, 16)
                nc.tensor.matmul(bank[4 + o][:, 0:D], dft_s, filt[:, o, :], start=True, stop=True)
                nc.tensor.matmul(bank[4 + o][:, D:2 * D], dft_c, filt[:, o, :], start=True, stop=True
                                 ).then_inc(spec_ps, 1)

            def transpose_ctx(loop, g, slot, chunks=range(DK)):
                pe.wait_ge(ld_raw[slot], raw_count(loop, g))
                for h in chunks:
                    if loop is not None or g >= 1:
                        pe.wait_ge(cTlo_rdy, twice(loop, 2 * (g - 1) + h + 1))
                    for t in range(tiles_of(g) if loop is None else GT):
                        last = nc.tensor.transpose(bank[h][:, t * P:(t + 1) * P],
                                                   raw[:, slot, t, h * P:(h + 1) * P], ident)
                    last.then_inc(cT_ps, 1)

            def scores(loop, g, n):
                pe.wait_ge(cTlo_rdy, twice(loop, 2 * g + 2))
                if g == 0:
                    pe.wait_ge(q_rdy, 1)
                if g >= 2:
                    pe.wait_ge(prob_rdy, times(loop, g - 1))
                r = g % 2
                for h in range(DK):
                    nc.tensor.matmul(bank[2 + r][:, 0:n], q_hi[:, h, :], cT_hi[:, r, h, 0:n],
                                     start=(h == 0), stop=False)
                    nc.tensor.matmul(bank[2 + r][:, 0:n], q_hi[:, h, :], cT_lo[:, r, h, 0:n],
                                     start=False, stop=False)
                    last = nc.tensor.matmul(bank[2 + r][:, 0:n], q_lo[:, h, :], cT_hi[:, r, h, 0:n],
                                            start=False, stop=(h == DK - 1))
                last.then_inc(score_ps, 1)

            def transpose_prob(loop, g, nt):
                pe.wait_ge(prob_rdy, times(loop, g + 1))
                if g >= 2:
                    pe.wait_ge(pTlo_rdy, times(loop, g - 1))
                for t in range(nt):
                    last = nc.tensor.transpose(bank[4 + g % 2][:, t * P:(t + 1) * P],
                                               prob[:, g % 2, t * P:(t + 1) * P], ident)
                last.then_inc(pT_ps, 1)

            def weigh(loop, g, slot, nt):
                pe.wait_ge(pTlo_rdy, times(loop, g + 1))
                pe.wait_ge(clo_rdy, times(loop, g + 1))
                if loop is not None or g >= 2:
                    pe.wait_ge(O_upd, times(loop, g - 1))
                r = g % 2
                for t in range(nt):
                    ph, pl = pT_hi[:, r, t * P:(t + 1) * P], pT_lo[:, r, t * P:(t + 1) * P]
                    nc.tensor.matmul(bank[6 + r][:, 0:D], ph, c_hi[:, slot, t, :],
                                     start=(t == 0), stop=False)
                    nc.tensor.matmul(bank[6 + r][:, 0:D], ph, c_lo[:, slot, t, :],
                                     start=False, stop=False)
                    last = nc.tensor.matmul(bank[6 + r][:, 0:D], pl, c_hi[:, slot, t, :],
                                            start=False, stop=(t == nt - 1))
                last.then_inc(pv_ps, 1)

            def step(loop, i):
                if i + 1 < GROUPS:
                    transpose_ctx(loop, i + 1, (i + 1) % RING)
                if i < GROUPS:
                    scores(loop, i, GT * P if loop is not None else tiles_of(i) * P)
                if 1 <= i <= GROUPS:
                    transpose_prob(loop, i - 1, GT if loop is not None else tiles_of(i - 1))
                if i >= 2:
                    weigh(loop, i - 2, (i - 2) % RING, GT if loop is not None else tiles_of(i - 2))

            transpose_ctx(None, 0, 0, (0,))
            pe.wait_ge(WT_rdy, DK)
            pe.wait_ge(xhT_rdy, 1)
            for e in range(DK):
                for d in range(DK):
                    last = nc.tensor.matmul(bank[(2, 5)[e]][:, 0:P], WT[:, d, e * P:(e + 1) * P],
                                            xhT[:, d, :], start=(d == 0), stop=(d == DK - 1))
                last.then_inc(exT_ps, 1)

            transpose_ctx(None, 0, 0, (1,))
            pe.wait_ge(exT_rdy, DK)
            for d in range(DK):
                for e in range(DK):
                    nc.tensor.matmul(bank[3][:, d * P:(d + 1) * P], W_sb[:, e, d * P:(d + 1) * P],
                                     exT[:, e, :], start=(e == 0), stop=(e == DK - 1))
            for e in range(DK):
                last = nc.tensor.matmul(bank[3][:, 2 * P:2 * P + 1], exT[:, e, :], col[:, 0, e:e + 1],
                                        start=(e == 0), stop=(e == DK - 1))
            last.then_inc(q_ps, 1)
            for i in range(FIRST):
                step(None, i)
            with pe.Fori(0, LOOPS) as n:
                for u in range(RING):
                    step(n, FIRST + u)
            for i in range(FIRST + RING * LOOPS, GROUPS + 2):
                step(None, i)

            pe.wait_ge(pTlo_rdy, GROUPS)
            for o in range(ORDER):
                spectrum(o)
            keep_busy(2)
            transpose_xh(pe, 1)
            keep_busy(4)
            pe.wait_ge(xhT_rdy, 2)
            pe.wait_ge(ld_pw, 32)

            def project(lo, hi, b):
                for k in range(DK):
                    last = nc.tensor.matmul(bank[b][:, 0:hi - lo], xhT[:, k, :], pw[:, k, lo:hi],
                                            start=(k == 0), stop=(k == DK - 1))
                last.then_inc(proj_ps, 1)

            def transpose_slots(n):
                k, half = n // 2, n % 2
                pe.wait_ge(se_rdy, 2 + half)
                if n == 3:
                    pe.wait_ge(seT_rdy, 1)
                for j in range(4):
                    last = nc.tensor.transpose(bank[SE_BANK[n]][:, j * P:(j + 1) * P],
                                               se[:, 4 * half + j, k * P:(k + 1) * P], ident)
                last.then_inc(seT_ps, 1)

            project(0, D, 2)
            project(D, 2 * D, 3)
            pe.wait_ge(spec_rdy, 2 * ORDER)
            for o in range(ORDER):
                pe.wait_ge(v_rdy, o + 1)
                for dft, b in ((dft_c, 4), (dft_s, 1)):
                    nc.tensor.matmul(bank[b][:, 0:D], dft, vbuf[:, o, :], start=True, stop=True
                                     ).then_inc(freq_ps, 1)
                for i, inv in enumerate((inv_s, inv_c, inv_s, inv_c)):
                    pe.wait_ge(prod_rdy, 4 * o + i + 1)
                    last = nc.tensor.matmul(bank[5][:, 0:D], inv, prod[:, i, :], start=(i == 0), stop=(i == 3))
                last.then_inc(conv_ps, 1)
                if o == 0:
                    project(2 * D, 3 * D, 7)
                else:
                    for n in range(4):
                        transpose_slots(n)
                    keep_busy(6)

            pe.wait_ge(z_rdy, 1)
            for k in range(DK):
                last = nc.tensor.transpose(bank[(7, 1)[k]][:, k * P:(k + 1) * P], xh[:, k * P:(k + 1) * P], ident)
            last.then_inc(zT_ps, 1)
            keep_busy(4)
            pe.wait_ge(xnT_rdy, DK)
            pe.wait_ge(seT_rdy, 4)

            def logits(n):
                lo, hi = PIECES[n]
                for k in range(DK):
                    last = nc.tensor.matmul(bank[3 + n][:, 0:(hi - lo) * P], xnT[:, k, :],
                                            seT[:, k, lo * P:hi * P], start=(k == 0), stop=(k == DK - 1))
                last.then_inc(L_ps, 1)

            def transpose_logits(n):
                lo, hi = PIECES[n]
                pe.wait_ge(L_rdy, n + 1)
                for c in range(lo, hi):
                    last = nc.tensor.transpose(bank[LT_BANK[n]][:, (c - lo) * P:(c - lo + 1) * P],
                                               comb[:, c * P:(c + 1) * P], ident)
                last.then_inc(LT_ps, 1)

            def transpose_dispatch(n):
                lo, hi = PIECES[n]
                pe.wait_ge(dT_rdy, n + 1)
                for c in range(lo, hi):
                    last = nc.tensor.transpose(bank[DISP_BANK[n]][:, (c - lo) * P:(c - lo + 1) * P],
                                               dT[:, c, :], ident)
                last.then_inc(disp_ps, 1)

            def gather(n):
                lo, hi = PIECES[n]
                pe.wait_ge(disp_rdy, n + 1)
                pe.wait_ge(xn_rdy, 1)
                for k in range(DK):
                    b, at = SLOTS_AT[n][k]
                    nc.tensor.matmul(bank[b][:, at:at + (hi - lo) * P], xn[:, k * P:(k + 1) * P],
                                     disp[:, lo * P:hi * P], start=True, stop=True).then_inc(slots_ps, 1)

            def combine_transpose(half):
                pe.wait_ge(cexp_rdy, half + 1)
                if half == 1:
                    pe.wait_ge(combT_rdy, 1)
                for j in range(4):
                    c = 4 * half + j
                    last = nc.tensor.transpose(bank[5][:, j * P:(j + 1) * P], comb[:, c * P:(c + 1) * P], ident)
                last.then_inc(combT_ps, 1)

            logits(0)
            keep_busy(2)
            transpose_logits(0)
            logits(1)
            transpose_dispatch(0)
            logits(2)
            transpose_logits(1)
            gather(0)
            transpose_logits(2)

            def hidden_of(p, which, b, done):
                s = p % WSLOTS
                if p < EARLY:
                    pe.wait_ge(ld_early, 16 * 3 * FEED)
                else:
                    pe.wait_ge(ld_wgu[s], 32)
                for k in range(DK):
                    for a in range(2):
                        last = nc.tensor.matmul(bank[b][a * SL:(a + 1) * SL, :],
                                                slotsT[:, k, p * P + a * SL:p * P + (a + 1) * SL],
                                                w_gu(s, which, a, a + 1)[:, 0, k, :], start=(k == 0), stop=(k == DK - 1))
                last.then_inc(done, 1)

            def down_of(p):
                s = p % WSLOTS
                pe.wait_ge(hidT_rdy, p + 1)
                if p >= EARLY:
                    pe.wait_ge(ld_wd[s], 16)
                if p >= 1:
                    pe.wait_ge(eout_rdy, p)
                for c in range(FC):
                    for a in range(2):
                        last = nc.tensor.matmul(bank[4][a * SL:(a + 1) * SL, 0:D],
                                                hidT[:, c, a * SL:(a + 1) * SL], w_d(s, a, a + 1)[:, 0, c, :],
                                                start=(c == 0), stop=(c == FC - 1))
                last.then_inc(down_ps, 1)

            def hidden_transpose(p):
                pe.wait_ge(hid_rdy, p + 1)
                if p >= 1:
                    pe.wait_ge(hidT_rdy, p)
                for c in range(FC):
                    last = nc.tensor.transpose(bank[3][:, c * P:(c + 1) * P], hid[:, c * P:(c + 1) * P], ident)
                last.then_inc(hidT_ps, 1)

            def mix_of(p):
                pe.wait_ge(eout_rdy, p + 1)
                if p == 0:
                    pe.wait_ge(combT_rdy, 2)
                last = nc.tensor.matmul(bank[1][:, 0:D], combT[:, p, :], eout[:, p % 2, :],
                                        start=(p == 0), stop=(p == PAIRS - 1))
                last.then_inc(mix_ps, 1)

            for p in range(PAIRS + 1):
                if p < PAIRS:
                    if p in (0, 1, 4):
                        pe.wait_ge(slots_rdy, {0: 1, 1: 3, 4: 5}[p])
                    if p >= 2:
                        pe.wait_ge(gate_rdy, p - 1)
                    hidden_of(p, 0, (6, 7)[p % 2], gate_ps)
                if p == 0:
                    transpose_dispatch(1)
                if p == 2:
                    pe.wait_ge(slots_rdy, 5)
                    combine_transpose(0)
                if p >= 1:
                    hidden_transpose(p - 1)
                if p < PAIRS:
                    if p >= 2:
                        pe.wait_ge(up_rdy, p - 1)
                    hidden_of(p, 1, UP_BANK[p % 2], up_ps)
                if p <= 1:
                    gather(p + 1)
                if p == 0:
                    transpose_dispatch(2)
                if p == 2:
                    combine_transpose(1)
                if p == PAIRS:
                    mix_of(p - 3)
                if p >= 1:
                    down_of(p - 1)
                if p >= 2 and p != PAIRS - 1:
                    mix_of(p - 2)
            mix_of(PAIRS - 1)

        @block.scalar
        def _(act):
            act.dma_start(ident, tables[:, 0, :]).then_inc(ld_ident, 16)
            act.dma_start(col[:, :, :], columns).then_inc(ld_col, 16)
            act.dma_start(scale_b[:, :], scale.rearrange("(a n) -> a n", a=1).broadcast_to([P, 1])
                          ).then_inc(ld_scale, 16)
            act.wait_ge(WT_ps, 1)
            nc.scalar.activation(WT[:, 0, :], bank[6][:, 0:D], ACT.Copy).then_inc(WT_rdy, 1)
            for h in range(DK):
                act.wait_ge(cT_ps, h + 1)
                nc.scalar.activation(cT_hi[:, 0, h, :], bank[h][:, :], ACT.Copy).then_inc(cThi_rdy, 1)
                if h == 0:
                    act.wait_ge(ld_col, 16)
                    act.wait_ge(exT_ps, 2)
                    nc.scalar.activation(exT[:, 1, :], bank[5][:, 0:P], ACT.Identity, bias=col[:, 0, 1:2]
                                         ).then_inc(exT_rdy, 1)
            act.wait_ge(q_ps, 1)
            nc.scalar.activation(q_hi[:, :, :].rearrange("p k q -> p (k q)"), bank[3][:, 0:D], ACT.Copy
                                 ).then_inc(qhi_rdy, 1)
            def spectrum(o):
                act.wait_ge(spec_ps, o + 1)
                nc.scalar.activation(spec[:, o, 0:2, :].rearrange("p a d -> p (a d)"), bank[4 + o][:, :], ACT.Copy
                                     ).then_inc(spec_rdy, 1)
                nc.scalar.activation(spec[:, o, 2, :], bank[4 + o][:, 0:D], ACT.Copy, scale=-1.0
                                     ).then_inc(spec_rdy, 1)

            def ctx_hi(loop, g, n):
                for h in range(DK):
                    act.wait_ge(cT_ps, twice(loop, 2 * g + h + 1))
                    if g >= 2:
                        act.wait_ge(score_ps, times(loop, g - 1))
                    nc.scalar.activation(cT_hi[:, g % 2, h, 0:n], bank[h][:, 0:n], ACT.Copy
                                         ).then_inc(cThi_rdy, 1)

            def rows_hi(loop, g, slot, nt):
                act.wait_ge(ld_raw[slot], raw_count(loop, g))
                if loop is not None or g >= RING:
                    act.wait_ge(pv_ps, times(loop, g - RING + 1))
                nc.scalar.activation(c_hi[:, slot, nt // 2:nt, :], raw[:, slot, nt // 2:nt, :], ACT.Copy
                                     ).then_inc(chi2_rdy, 1)

            def prob_hi(loop, g, n):
                act.wait_ge(pT_ps, times(loop, g + 1))
                if g >= 2:
                    act.wait_ge(pv_ps, times(loop, g - 1))
                nc.scalar.activation(pT_hi[:, g % 2, 0:n], bank[4 + g % 2][:, 0:n], ACT.Copy
                                     ).then_inc(pThi_rdy, 1)

            def exps(loop, g, n):
                act.wait_ge(ebias_rdy, times(loop, g + 1))
                if g >= 2:
                    act.wait_ge(pT_ps, times(loop, g - 1))
                nc.scalar.activation(prob[:, g % 2, 0:n], bank[2 + g % 2][:, 0:n], ACT.Exp,
                                     bias=ebias[:, g % RING:g % RING + 1],
                                     accum_out=rsum[:, g % RING:g % RING + 1]).then_inc(prob_rdy, 1)
                nc.scalar.activation(alpha[:, g % RING:g % RING + 1],
                                     negm[:, (g - 1) % RING:(g - 1) % RING + 1], ACT.Exp, scale=-1.0,
                                     bias=negm[:, g % RING:g % RING + 1]).then_inc(alpha_rdy, 1)

            def step(loop, i):
                full = loop is not None
                if i + 1 < GROUPS:
                    ctx_hi(loop, i + 1, (GT if full else tiles_of(i + 1)) * P)
                    rows_hi(loop, i + 1, (i + 1) % RING, GT if full else tiles_of(i + 1))
                if 1 <= i <= GROUPS:
                    prob_hi(loop, i - 1, (GT if full else tiles_of(i - 1)) * P)
                if i < GROUPS:
                    exps(loop, i, (GT if full else tiles_of(i)) * P)

            rows_hi(None, 0, 0, GT)
            ctx_hi(None, 1, GT * P)
            rows_hi(None, 1, 1, GT)
            ctx_hi(None, 2, GT * P)
            exps(None, 0, GT * P)
            rows_hi(None, 2, 2, GT)
            prob_hi(None, 0, GT * P)
            exps(None, 1, GT * P)
            for i in range(2, FIRST):
                step(None, i)
            with act.Fori(0, LOOPS) as n:
                for u in range(RING):
                    step(n, FIRST + u)
            for i in range(FIRST + RING * LOOPS, GROUPS + 1):
                step(None, i)

            for o in range(ORDER):
                spectrum(o)
            act.wait_ge(gs_rdy, 1)
            for n in range(4):
                act.wait_ge(seT_ps, n + 1)
                k, half = n // 2, n % 2
                nc.scalar.activation(seT[:, k, half * 512:(half + 1) * 512], bank[SE_BANK[n]][:, :],
                                     ACT.Identity, scale=col[:, 1, k:k + 1], bias=col[:, 2, k:k + 1]
                                     ).then_inc(seT_rdy, 1)
            act.wait_ge(zT_ps, 1)
            k = 1
            nc.scalar.activation(xnT[:, k, :], bank[1][:, k * P:(k + 1) * P], ACT.Identity,
                                 scale=col[:, 3, k:k + 1], bias=col[:, 4, k:k + 1]).then_inc(xnT_rdy, 1)

            def copy_logits(n):
                lo, hi = PIECES[n]
                act.wait_ge(L_ps, n + 1)
                act.wait_ge(L_rdy, n)
                nc.scalar.activation(comb[:, lo * P:hi * P], bank[3 + n][:, 0:(hi - lo) * P], ACT.Copy
                                     ).then_inc(L_rdy, 1)

            def exp_dispatch(n):
                lo, hi = PIECES[n]
                act.wait_ge(cmax_rdy, n + 1)
                for c in range(lo, hi):
                    last = nc.scalar.activation(dT[:, c, :], bank[LT_BANK[n]][:, (c - lo) * P:(c - lo + 1) * P],
                                                ACT.Exp, bias=cmax[:, c:c + 1], accum_out=csum[:, c:c + 1])
                last.then_inc(dexp_rdy, 1)

            def copy_slots(n):
                lo, hi = PIECES[n]
                b, at = SLOTS_AT[n][1]
                act.wait_ge(slots_ps, 2 * n + 2)
                nc.scalar.activation(slotsT[:, 1, lo * P:hi * P], bank[b][:, at:at + (hi - lo) * P], ACT.Copy
                                     ).then_inc(slots_rdy, 1)

            exp_dispatch(0)
            copy_logits(1)
            copy_logits(2)
            exp_dispatch(1)
            exp_dispatch(2)

            def combine_copy(half):
                act.wait_ge(combT_ps, half + 1)
                act.wait_ge(disp_ps, 3)
                nc.scalar.activation(combT[:, 4 * half:4 * half + 4, :].rearrange("p j n -> p (j n)"),
                                     bank[5][:, :], ACT.Copy).then_inc(combT_rdy, 1)

            for p in range(PAIRS):
                act.wait_ge(gate_rdy, p + 1)
                nc.scalar.activation(gate[:, p % 2, :], gate[:, p % 2, :], ACT.Gelu).then_inc(gelu_rdy, 1)
                if p <= 1:
                    copy_slots(p + 1)
                if p == 1:
                    act.wait_ge(rmax_rdy, 1)
                    act.wait_ge(LT_ps, 3)
                    for half in range(2):
                        nc.scalar.activation(comb[:, half * 512:(half + 1) * 512],
                                             comb[:, half * 512:(half + 1) * 512], ACT.Exp, bias=rmax[:, 0:1],
                                             accum_out=rs[:, half:half + 1]).then_inc(cexp_rdy, 1)
                    combine_copy(0)
                if p == 2:
                    combine_copy(1)
                act.wait_ge(hidT_ps, p + 1)
                if p >= 1:
                    act.wait_ge(down_ps, p)
                nc.scalar.activation(hidT[:, :, :].rearrange("p c s -> p (c s)"), bank[3][:, :], ACT.Copy
                                     ).then_inc(hidT_rdy, 1)

        @block.gpsimd
        def _(pool):
            nc.gpsimd.memset(neg_half[:, :], -0.5).then_inc(const_set, 1)
            nc.gpsimd.memset(zero[:, :], 0.0).then_inc(const_set, 1)
            pool.wait_ge(const_set, 2)

            def power(n, dst, src, width):
                pool.wait_ge(var_rdy, n + 1)
                nc.gpsimd.tensor_tensor(dst, src, neg_half[:, 0:width], ALU.pow).then_inc(rstd_rdy, 1)

            power(0, rstd[:, 0:1], mv[:, 1:2], 1)

            def split_ctx(loop, g, slot, nt):
                pool.wait_ge(ld_raw[slot], raw_count(loop, g))
                if loop is not None or g >= RING:
                    pool.wait_ge(pv_ps, times(loop, g - RING + 1))
                nc.gpsimd.tensor_tensor(c_hi[:, slot, 0:nt // 2, :].rearrange("p t d -> p (t d)"),
                                        raw[:, slot, 0:nt // 2, :].rearrange("p t d -> p (t d)"),
                                        zero[:, 0:1].broadcast_to([P, nt // 2 * D]), ALU.add).then_inc(chi_rdy, 1)
                pool.wait_ge(chi_rdy, times(loop, g + 1))
                pool.wait_ge(chi2_rdy, times(loop, g + 1))
                nc.gpsimd.tensor_tensor(c_lo[:, slot, 0:nt, :], raw[:, slot, 0:nt, :],
                                        c_hi[:, slot, 0:nt, :].bitcast(fp32), ALU.subtract
                                        ).then_inc(clo_rdy, 1)

            for g in range(RING):
                split_ctx(None, g, g, GT)
            with pool.Fori(0, LOOPS) as n:
                for u in range(RING):
                    split_ctx(n, RING + u, u, GT)
            split_ctx(None, LAST, LAST % RING, LAST_T)
            power(1, rstd[:, 0:1], mv[:, 1:2], 1)
            power(2, se_rstd[:, :], se_mv[:, :, 1], PAIRS)
            power(3, rstd[:, 0:1], mv[:, 1:2], 1)

        @block.vector
        def _(dve):
            count = [0]

            def link(ins):
                count[0] += 1
                ins.then_inc(dve_n, 1)
                dve.wait_ge(dve_n, count[0])

            def mean_and_variance(src):
                link(nc.vector.bn_stats(stat6[:, :], src))
                link(nc.vector.bn_aggr(mv[:, :], stat6[:, :]))

            def norm(n, src, dst, done):
                mean_and_variance(src)
                nc.vector.tensor_scalar(mv[:, 1:2], mv[:, 1:2], EPS, None, ALU.add).then_inc(var_rdy, 1)
                dve.wait_ge(rstd_rdy, n + 1)
                nc.vector.tensor_scalar(dst, src, mv[:, 0:1], rstd[:, 0:1], ALU.subtract, ALU.mult
                                        ).then_inc(done, 1)

            nc.vector.memset(O[:, :], 0.0).then_inc(idle_set, 1)
            nc.vector.memset(negm[:, RING - 1:RING], BIG)
            nc.vector.memset(lsum[:, :], 0.0)
            dve.wait_ge(ld_x, 16)
            norm(0, x_sb[:, :], xh[:, :], xh_rdy)
            dve.wait_ge(WT_ps, 2)
            nc.vector.tensor_copy(WT[:, 1, :], bank[7][:, 0:D]).then_inc(WT_rdy, 1)
            dve.wait_ge(xhT_ps, 1)
            nc.vector.tensor_copy(xhT[:, :, :].rearrange("p k t -> p (k t)"), bank[XH_BANK[0]][:, 0:D]).then_inc(xhT_rdy, 1)
            dve.wait_ge(ld_col, 16)
            dve.wait_ge(exT_ps, 1)
            nc.vector.tensor_scalar(exT[:, 0, :], bank[2][:, 0:P], col[:, 0, 0:1], None, ALU.add
                                    ).then_inc(exT_rdy, 1)
            dve.wait_ge(ld_scale, 16)
            for i in (1, 2):
                last = nc.vector.tensor_scalar(col[:, i, :], col[:, i, :], scale_b[:, 0:1], None, ALU.mult)
            last.then_inc(gs_rdy, 1)

            def slot_stats(loop, j):
                if loop is None:
                    if j == 0:
                        dve.wait_ge(ld_se, 16)
                    nc.vector.bn_stats(se_stat[:, j, :], se[:, j, :]).then_inc(stat_rdy, 1)
                else:
                    nc.vector.bn_stats(se_stat[:, bass.ds(loop + j, 1), :].rearrange("p j s -> p (j s)"),
                                       se[:, bass.ds(loop + j, 1), :].rearrange("p j d -> p (j d)")
                                       ).then_inc(stat_rdy, 1)

            def slot_variance():
                dve.wait_ge(stat_rdy, PAIRS)
                for j in range(PAIRS):
                    last = nc.vector.bn_aggr(se_mv[:, j, :], se_stat[:, j, :])
                link(last)
                nc.vector.tensor_scalar(se_mv[:, :, 1], se_mv[:, :, 1], EPS, None, ALU.add).then_inc(var_rdy, 1)

            def slot_norm(lo, hi):
                for j in range(lo, hi):
                    last = nc.vector.tensor_scalar(se[:, j, :], se[:, j, :], se_mv[:, j, 0:1],
                                                   se_rstd[:, j:j + 1], ALU.subtract, ALU.mult)
                last.then_inc(se_rdy, 1)

            def ctx_lo(loop, g, n):
                for h in range(DK):
                    dve.wait_ge(cThi_rdy, twice(loop, 2 * g + h + 1))
                    nc.vector.tensor_tensor(cT_lo[:, g % 2, h, 0:n], bank[h][:, 0:n],
                                            cT_hi[:, g % 2, h, 0:n].bitcast(fp32), ALU.subtract
                                            ).then_inc(cTlo_rdy, 1)

            def running_max(loop, g, n):
                r = g % RING
                dve.wait_ge(score_ps, times(loop, g + 1))
                nc.vector.tensor_reduce(gmax[:, :], bank[2 + g % 2][:, 0:n], AX.X, ALU.max, negate=True
                                        ).then_inc(gmax_rdy, 1)
                dve.wait_ge(gmax_rdy, times(loop, g + 1))
                nc.vector.scalar_tensor_tensor(out=negm[:, r:r + 1], in0=gmax[:, :], scalar=s0[:, 0:1],
                                               in1=negm[:, (g - 1) % RING:(g - 1) % RING + 1],
                                               op0=ALU.subtract, op1=ALU.min).then_inc(negm_rdy, 1)
                dve.wait_ge(negm_rdy, times(loop, g + 1))
                nc.vector.tensor_tensor(ebias[:, r:r + 1], negm[:, r:r + 1], s0[:, :], ALU.add
                                        ).then_inc(ebias_rdy, 1)

            def prob_lo(loop, g, n):
                dve.wait_ge(pThi_rdy, times(loop, g + 1))
                nc.vector.tensor_tensor(pT_lo[:, g % 2, 0:n], bank[4 + g % 2][:, 0:n],
                                        pT_hi[:, g % 2, 0:n].bitcast(fp32), ALU.subtract).then_inc(pTlo_rdy, 1)

            def update_sum(loop, g):
                r = g % RING
                dve.wait_ge(alpha_rdy, times(loop, g + 1))
                if g >= 1:
                    dve.wait_ge(l_upd, times(loop, g))
                nc.vector.scalar_tensor_tensor(out=lsum[:, :], in0=lsum[:, :], scalar=alpha[:, r:r + 1],
                                               in1=rsum[:, r:r + 1], op0=ALU.mult, op1=ALU.add).then_inc(l_upd, 1)

            def update_output(loop, g):
                r = g % RING
                dve.wait_ge(pv_ps, times(loop, g + 1))
                if g >= 1:
                    dve.wait_ge(O_upd, times(loop, g))
                nc.vector.scalar_tensor_tensor(out=O[:, :], in0=O[:, :], scalar=alpha[:, r:r + 1],
                                               in1=bank[6 + g % 2][:, 0:D], op0=ALU.mult, op1=ALU.add
                                               ).then_inc(O_upd, 1)

            def step(loop, i):
                full = loop is not None
                if i + 1 < GROUPS:
                    ctx_lo(loop, i + 1, (GT if full else tiles_of(i + 1)) * P)
                if i < GROUPS:
                    running_max(loop, i, (GT if full else tiles_of(i)) * P)
                if 1 <= i <= GROUPS:
                    prob_lo(loop, i - 1, (GT if full else tiles_of(i - 1)) * P)
                if i >= 2:
                    update_sum(loop, i - 2)
                    if i - 2 < LAST - 1:
                        update_output(loop, i - 2)

            ctx_lo(None, 0, GT * P)
            dve.wait_ge(qhi_rdy, 1)
            nc.vector.tensor_tensor(q_lo[:, :, :].rearrange("p k q -> p (k q)"), bank[3][:, 0:D],
                                    q_hi[:, :, :].rearrange("p k q -> p (k q)").bitcast(fp32), ALU.subtract
                                    ).then_inc(q_rdy, 1)
            nc.vector.tensor_copy(s0[:, :], bank[3][:, 2 * P:2 * P + 1]).then_inc(s0_rdy, 1)
            dve.wait_ge(s0_rdy, 1)
            for i in range(FIRST):
                step(None, i)
                slot_stats(None, i)
            with dve.Fori(0, LOOPS) as n:
                for u in range(RING):
                    step(n, FIRST + u)
                    if u == 0:
                        slot_stats(n, FIRST)
            for i in range(FIRST + RING * LOOPS, GROUPS + 2):
                step(None, i)

            r = LAST % RING
            dve.wait_ge(l_upd, GROUPS)
            link(nc.vector.reciprocal(linv[:, :], lsum[:, :]))
            link(nc.vector.tensor_tensor(alpha[:, r:r + 1], alpha[:, r:r + 1], linv[:, :], ALU.mult))
            update_output(None, LAST - 1)
            dve.wait_ge(O_upd, LAST)
            link(nc.vector.scalar_tensor_tensor(out=x1[:, :], in0=O[:, :], scalar=alpha[:, r:r + 1], in1=x_sb[:, :],
                                                op0=ALU.mult, op1=ALU.add))
            dve.wait_ge(pv_ps, GROUPS)
            link(nc.vector.scalar_tensor_tensor(out=x1[:, :], in0=bank[6 + LAST % 2][:, 0:D], scalar=linv[:, 0:1],
                                                in1=x1[:, :], op0=ALU.mult, op1=ALU.add))
            norm(1, x1[:, :], xh[:, :], xh_rdy)
            slot_variance()
            dve.wait_ge(xhT_ps, 2)
            nc.vector.tensor_copy(xhT[:, :, :].rearrange("p k t -> p (k t)"), bank[XH_BANK[1]][:, 0:D]).then_inc(xhT_rdy, 1)
            dve.wait_ge(ld_pw, 32)
            dve.wait_ge(proj_ps, 1)
            nc.vector.tensor_tensor(vbuf[:, 0, :], bank[2][:, 0:D], pb[:, 0:D], ALU.add).then_inc(v_rdy, 1)
            dve.wait_ge(rstd_rdy, 3)
            slot_norm(0, 2)
            for o in range(ORDER):
                for i, f in enumerate((0, 1, 1, 2)):
                    dve.wait_ge(freq_ps, 2 * o + i // 2 + 1)
                    nc.vector.tensor_tensor(prod[:, i, :], bank[(4, 1)[i // 2]][:, 0:D], spec[:, o, f, :], ALU.mult
                                            ).then_inc(prod_rdy, 1)
                if o == 0:
                    dve.wait_ge(proj_ps, 2)
                    link(nc.vector.tensor_tensor(p_sb[:, D:2 * D], bank[3][:, 0:D], pb[:, D:2 * D], ALU.add))
                slot_norm(*((2, 5), (5, PAIRS))[o])
                dve.wait_ge(conv_ps, o + 1)
                if o + 1 < ORDER:
                    nc.vector.tensor_tensor(vbuf[:, o + 1, :], bank[5][:, 0:D], p_sb[:, (o + 1) * D:(o + 2) * D],
                                            ALU.mult).then_inc(v_rdy, 1)
                    dve.wait_ge(proj_ps, 3)
                    link(nc.vector.tensor_tensor(p_sb[:, 2 * D:3 * D], bank[7][:, 0:D], pb[:, 2 * D:3 * D],
                                                 ALU.add))
                else:
                    link(nc.vector.tensor_tensor(xn[:, :], bank[5][:, 0:D], p_sb[:, (o + 1) * D:(o + 2) * D],
                                                 ALU.mult))
            link(nc.vector.tensor_tensor(x2[:, :], x1[:, :], xn[:, :], ALU.add))
            mean_and_variance(x2[:, :])
            nc.vector.tensor_scalar(mv[:, 1:2], mv[:, 1:2], 1.0 + EPS, EPS * EPS, ALU.mult, ALU.add
                                    ).then_inc(var_rdy, 1)
            dve.wait_ge(rstd_rdy, 4)
            nc.vector.tensor_scalar(xh[:, :], x2[:, :], mv[:, 0:1], rstd[:, 0:1], ALU.subtract, ALU.mult
                                    ).then_inc(z_rdy, 1)
            dve.wait_ge(ld_row, 32)
            dve.wait_ge(z_rdy, 1)
            dve.wait_ge(zT_ps, 1)
            nc.vector.tensor_scalar(xnT[:, 0, :], bank[7][:, 0:P], col[:, 3, 0:1], col[:, 4, 0:1],
                                    ALU.mult, ALU.add).then_inc(xnT_rdy, 1)
            link(nc.vector.tensor_tensor(xn[:, :], xh[:, :], g_row[:, 0, :], ALU.mult))
            nc.vector.tensor_tensor(xn[:, :], xn[:, :], g_row[:, 1, :], ALU.add).then_inc(xn_rdy, 1)

            def dispatch_max(n):
                lo, hi = PIECES[n]
                dve.wait_ge(LT_ps, n + 1)
                nc.vector.tensor_reduce(cmax[:, lo:hi],
                                        bank[LT_BANK[n]][:, 0:(hi - lo) * P].rearrange("p (j n) -> p j n", n=P),
                                        AX.X, ALU.max, negate=True).then_inc(cmax_rdy, 1)

            def dispatch_norm(n):
                lo, hi = PIECES[n]
                dve.wait_ge(dexp_rdy, n + 1)
                link(nc.vector.reciprocal(cinv[:, lo:hi], csum[:, lo:hi]))
                nc.vector.tensor_tensor(dT[:, lo:hi, :], dT[:, lo:hi, :],
                                        cinv[:, lo:hi].unsqueeze(2).broadcast_to([P, hi - lo, P]), ALU.mult
                                        ).then_inc(dT_rdy, 1)

            def dispatch_copy(n):
                lo, hi = PIECES[n]
                dve.wait_ge(disp_ps, n + 1)
                nc.vector.tensor_copy(disp[:, lo * P:hi * P], bank[DISP_BANK[n]][:, 0:(hi - lo) * P]
                                      ).then_inc(disp_rdy, 1)

            def copy_slots(n):
                lo, hi = PIECES[n]
                b, at = SLOTS_AT[n][0]
                if n == 0:
                    dve.wait_ge(slots_ps, 2)
                    nc.vector.tensor_copy(slotsT[:, :, lo * P:hi * P],
                                          bank[b][:, 0:DK * P].rearrange("p (k s) -> p k s", k=DK)
                                          ).then_inc(slots_rdy, 1)
                else:
                    dve.wait_ge(slots_ps, 2 * n + 1)
                    nc.vector.tensor_copy(slotsT[:, 0, lo * P:hi * P], bank[b][:, at:at + (hi - lo) * P]
                                          ).then_inc(slots_rdy, 1)

            dve.wait_ge(L_ps, 1)
            nc.vector.tensor_copy(comb[:, 0:P], bank[3][:, 0:P]).then_inc(L_rdy, 1)
            dispatch_max(0)
            dispatch_norm(0)
            dispatch_copy(0)
            dispatch_max(1)
            copy_slots(0)
            dispatch_max(2)
            dispatch_norm(1)
            for p in range(PAIRS + 1):
                if p < PAIRS:
                    dve.wait_ge(ld_bias[p % BSLOTS], 32 * (p // BSLOTS + 1))
                    dve.wait_ge(gate_ps, p + 1)
                    if p >= 2:
                        dve.wait_ge(hid_rdy, p - 1)
                    nc.vector.tensor_tensor(gate[:, p % 2, :], bank[(6, 7)[p % 2]][:, :],
                                            bias[:, p % BSLOTS, 0:F], ALU.add
                                            ).then_inc(gate_rdy, 1)
                    if p == 0:
                        dispatch_copy(1)
                        dispatch_norm(2)
                    dve.wait_ge(up_ps, p + 1)
                    if p >= 1:
                        dve.wait_ge(hid_rdy, p)
                    nc.vector.tensor_tensor(up[:, :], bank[UP_BANK[p % 2]][:, :],
                                            bias[:, p % BSLOTS, F:2 * F], ALU.add
                                            ).then_inc(up_rdy, 1)
                    if p == 0:
                        copy_slots(1)
                        dispatch_copy(2)
                    dve.wait_ge(up_rdy, p + 1)
                    dve.wait_ge(gelu_rdy, p + 1)
                    if p >= 1:
                        dve.wait_ge(hidT_ps, p)
                    nc.vector.tensor_tensor(hid[:, :], gate[:, p % 2, :], up[:, :], ALU.mult).then_inc(hid_rdy, 1)
                    if p == 1:
                        copy_slots(2)
                        dve.wait_ge(L_rdy, 3)
                        nc.vector.tensor_reduce(rmax[:, :], comb[:, :], AX.X, ALU.max, negate=True
                                                ).then_inc(rmax_rdy, 1)
                if p == 2:
                    dve.wait_ge(cexp_rdy, 2)
                    link(nc.vector.tensor_tensor(rs[:, 2:3], rs[:, 0:1], rs[:, 1:2], ALU.add))
                    link(nc.vector.reciprocal(rs[:, 3:4], rs[:, 2:3]))
                if p >= 1:
                    dve.wait_ge(down_ps, p)
                    if p >= 3:
                        dve.wait_ge(mix_ps, p - 2)
                    nc.vector.tensor_tensor(eout[:, (p - 1) % 2, :], bank[4][:, 0:D],
                                            bias[:, (p - 1) % BSLOTS, 2 * F:2 * F + D], ALU.add
                                            ).then_inc(eout_rdy, 1)
            dve.wait_ge(mix_ps, PAIRS)
            nc.vector.scalar_tensor_tensor(out=x1[:, :], in0=bank[1][:, 0:D], scalar=rs[:, 3:4], in1=x2[:, :],
                                           op0=ALU.mult, op1=ALU.add).then_inc(res_rdy, 1)


def spectrum_tables(np, n):
    t = np.arange(n)[:, None]
    w = 2.0 * np.pi * (np.arange(n)[None, :] + 0.5) / (2 * n)
    c, s = np.cos(t * w), np.sin(t * w)
    return np.stack([np.eye(n), c, s, c.T / n, s.T / n], axis=1).astype(np.float32)


_INS = ['x', 'ctx_1024', 'L0_xattn_W', 'L0_attn_proj_w', 'L0_attn_proj_b', 'L0_attn_filter_time',
        'L0_ffn_norm_g', 'L0_ffn_norm_b', 'L0_ffn_scale', 'L0_ffn_slot_embeds', 'L0_ffn_Wg', 'L0_ffn_Wu', 'L0_ffn_Wd']


def kernel(**inputs):
    import numpy as _np
    import concourse.bacc as _bacc
    from concourse import mybir as _mybir
    from concourse.bass_utils import run_bass_kernel_spmd as _run

    nc = _bacc.Bacc("TRN2", target_bir_lowering=False, num_devices=1)
    arrays, args = {}, []

    def add(name, a):
        arrays[name] = a
        args.append(nc.dram_tensor(name, a.shape, _mybir.dt.from_np(a.dtype), kind="ExternalInput").ap())

    for name in _INS:
        add(f"in_{name}_dram", _np.ascontiguousarray(inputs[name]))
    add("biases_dram", _np.concatenate([_np.asarray(inputs[n]) for n in ('L0_ffn_bg', 'L0_ffn_bu', 'L0_ffn_bd')], 1))
    vectors = [inputs[n] for n in ('L0_xattn_b', 'L0_ffn_slot_g', 'L0_ffn_slot_b', 'L0_ffn_norm_g', 'L0_ffn_norm_b')]
    add("columns_dram", _np.ascontiguousarray(_np.stack(
        [_np.asarray(v).reshape(2, 128).transpose(1, 0) for v in vectors], axis=1)))
    add("tables_dram", spectrum_tables(_np, 128))
    args.append(nc.dram_tensor("out_0_dram", (1, 128, 256), _mybir.dt.from_np(_np.dtype("float32")),
                               kind="ExternalOutput").ap())
    perceiver_kernel(nc, *args)
    return _run(nc, [arrays], core_ids=[0]).results[0]["out_0_dram"]
```
